# Optimizing a Trainium2 kernel written in Bass

```python
import numpy as np
import jax
import jax.numpy as jnp

def _softmax(x, axis=-1):
    return jax.nn.softmax(x, axis=axis)

def _gelu(x):
    return jax.nn.gelu(x, approximate=True)

def _silu(x):
    return jax.nn.silu(x)

def _sigmoid(x):
    return jax.nn.sigmoid(x)

def _layernorm(x, axis=-1, eps=1e-05):
    m = jnp.mean(x, axis=axis, keepdims=True)
    v = jnp.var(x, axis=axis, keepdims=True)
    return (x - m) / jnp.sqrt(v + eps)

def _scatter_add(tgt, idx, src, axis=0):
    return tgt.at[idx].add(src)

def _segment_sum(src, seg, n):
    return jax.ops.segment_sum(src, seg, n)
kernel_name = 'mk_gnn_preln_d1_gnn_r8_2c2952'

def setup_inputs(seed: int=0):
    np.random.seed(seed)
    _w = jnp.asarray

    def _rec_inputs():
        import jax
        import jax.numpy as jnp
        _gk = jax.random.key(seed)
        x = -0.0003713 + 1 * jax.random.normal(jax.random.fold_in(_gk, 1), (6250, 128), jnp.float32)
        _s = jax.random.randint(jax.random.fold_in(_gk, 2), (100000,), 0, 6250, jnp.int32)
        _d = jax.random.randint(jax.random.fold_in(_gk, 3), (100000,), 0, 6250, jnp.int32)
        _loop = jnp.arange(6250, dtype=jnp.int32)
        src = jnp.concatenate([_s, _d, _loop])
        dst = jnp.concatenate([_d, _s, _loop])
        _o = jnp.argsort(dst, stable=True)
        src = src[_o]
        dst = dst[_o]
        edge_attr_64 = -8.16379e-05 + 0.999858 * jax.random.normal(jax.random.fold_in(_gk, 12), (206250, 64), jnp.float32)
        return (x, src, dst, edge_attr_64)
    x, src, dst, edge_attr_64 = _rec_inputs()

    def _L0_gnn_setup():
        import jax, jax.numpy as jnp
        import numpy as np
        N_NODES = 12500
        N_EDGES = 200000
        NDIM_IN = 128
        EDIMS = 64
        NDIM_OUT = 128
        NUM_HEADS = 4
        HEAD_DIM = NDIM_OUT // NUM_HEADS
        key = jax.random.key(seed)
        ks = jax.random.split(key, 10)
        in_dim = NDIM_IN + EDIMS
        b1 = float(np.sqrt(6.0 / (in_dim + NDIM_OUT)))
        b2 = float(np.sqrt(6.0 / (NDIM_OUT + NDIM_OUT)))
        bav = float(np.sqrt(6.0 / (NUM_HEADS + HEAD_DIM)))
        return {'nfeats': jax.random.normal(ks[0], (N_NODES, NDIM_IN), dtype=jnp.float32), 'efeats': jax.random.normal(ks[1], (N_EDGES, EDIMS), dtype=jnp.float32), 'src': jax.random.randint(ks[2], (N_EDGES,), 0, N_NODES, dtype=jnp.int32), 'dst': jax.random.randint(ks[3], (N_EDGES,), 0, N_NODES, dtype=jnp.int32), 'W_proj_w': jax.random.uniform(ks[4], (NDIM_OUT, in_dim), jnp.float32, -b1, b1), 'W_proj_b': jnp.zeros((NDIM_OUT,), jnp.float32), 'attn_vec': jax.random.uniform(ks[5], (NUM_HEADS, HEAD_DIM), jnp.float32, -bav, bav), 'W_out_w': jax.random.uniform(ks[6], (NDIM_OUT, NDIM_OUT), jnp.float32, -b2, b2), 'W_out_b': jnp.zeros((NDIM_OUT,), jnp.float32), 'ln_gamma': jnp.ones((NDIM_OUT,), jnp.float32), 'ln_beta': jnp.zeros((NDIM_OUT,), jnp.float32)}
    _L0_gnn_all = _L0_gnn_setup()
    _L0_gnn_in = {k: v for k, v in _L0_gnn_all.items() if k in ('W_proj_w', 'W_proj_b', 'attn_vec', 'W_out_w', 'W_out_b', 'ln_gamma', 'ln_beta')}
    del _L0_gnn_all
    return {'x': x, 'src': src, 'dst': dst, 'edge_attr_64': edge_attr_64, 'L0_gnn_W_proj_w': _L0_gnn_in['W_proj_w'], 'L0_gnn_W_proj_b': _L0_gnn_in['W_proj_b'], 'L0_gnn_attn_vec': _L0_gnn_in['attn_vec'], 'L0_gnn_W_out_w': _L0_gnn_in['W_out_w'], 'L0_gnn_W_out_b': _L0_gnn_in['W_out_b'], 'L0_gnn_ln_gamma': _L0_gnn_in['ln_gamma'], 'L0_gnn_ln_beta': _L0_gnn_in['ln_beta']}

def reference(x, src, dst, edge_attr_64, L0_gnn_W_proj_w, L0_gnn_W_proj_b, L0_gnn_attn_vec, L0_gnn_W_out_w, L0_gnn_W_out_b, L0_gnn_ln_gamma, L0_gnn_ln_beta):
    import jax
    import jax.numpy as jnp

    def _L0_gnn_ref(nfeats, efeats, src, dst, W_proj_w, W_proj_b, attn_vec, W_out_w, W_out_b, ln_gamma, ln_beta):
        import jax, jax.numpy as jnp
        import numpy as np
        N_NODES = 12500
        N_EDGES = 200000
        NDIM_IN = 128
        EDIMS = 64
        NDIM_OUT = 128
        NUM_HEADS = 4
        HEAD_DIM = NDIM_OUT // NUM_HEADS
        N = nfeats.shape[0]
        H, D = attn_vec.shape
        x = jnp.concatenate([nfeats[src], efeats], axis=1)
        x_proj = (x @ W_proj_w.T + W_proj_b).reshape(-1, H, D)
        e = jnp.sum(x_proj * attn_vec, axis=-1)
        emax = jax.ops.segment_max(e, dst, num_segments=N)
        ex = jnp.exp(e - emax[dst])
        denom = jax.ops.segment_sum(ex, dst, num_segments=N)
        alpha = ex / denom[dst]
        m = (x_proj * alpha[:, :, None]).reshape(-1, H * D)
        h_neigh = jax.ops.segment_sum(m, dst, num_segments=N)
        h = jax.nn.relu((h_neigh + nfeats) @ W_out_w.T + W_out_b)
        mu = jnp.mean(h, axis=-1, keepdims=True)
        var = jnp.mean((h - mu) ** 2, axis=-1, keepdims=True)
        return (h - mu) * jax.lax.rsqrt(var + 1e-05) * ln_gamma + ln_beta
    h = jnp.maximum(_layernorm(x, axis=-1), 0.0)
    x = x + _L0_gnn_ref(h, edge_attr_64, src, dst, L0_gnn_W_proj_w, L0_gnn_W_proj_b, L0_gnn_attn_vec, L0_gnn_W_out_w, L0_gnn_W_out_b, L0_gnn_ln_gamma, L0_gnn_ln_beta)
    return x

_drawn_inputs = setup_inputs


def setup_inputs(seed=0):
    import zlib

    import numpy as np

    out = dict(_drawn_inputs(seed))
    spreads = {'L0_gnn_W_proj_b': (0.0, 0.1),
     'L0_gnn_W_out_b': (0.0, 0.1),
     'L0_gnn_ln_gamma': (1.0, 0.2),
     'L0_gnn_ln_beta': (0.0, 0.1)}
    factors = {}
    for name, (base, spread) in spreads.items():
        noise = np.random.default_rng([zlib.crc32(name.encode()), seed]).standard_normal(out[name].shape)
        drawn = base * np.exp(spread * noise) if base else spread * noise
        out[name] = jnp.asarray(drawn.astype(out[name].dtype))
    for name, factor in factors.items():
        out[name] = (out[name] * factor).astype(out[name].dtype)
    return out
```

```python
from contextlib import ExitStack

import concourse.bass as bass
from concourse import mybir

F32 = mybir.dt.float32
I32 = mybir.dt.int32
ALU = mybir.AluOpType
ACT = mybir.ActivationFunctionType
AX_X = mybir.AxisListType.X

P = 128
N, E, D, ED = 6250, 206250, 128, 64
H, HD = 4, 32
ROW = D + H
GT = 32
Q = 8
QT = GT // Q
WIN = 20
RING = 3
NT = -(-N // P)
NG = -(-NT // 4)
NPAD = NG * 4 * P
TILES = -(-E // P)
NS = -(-TILES // GT)
assert NS % RING == 0 and H * GT == P and Q * QT == GT and NG % 2 == 1
LOOPS = NS // RING - 1
LAST_TILES = TILES - (NS - 1) * GT
PAD_DST = N
LEAD_DST = N + 1
DST_ROWS = slice(0, P)
DST_COLS = slice(P, P + GT)
SRC_COLS = slice(P + GT, P + 2 * GT)
BOUNDS = slice(P + 2 * GT, P + 4 * GT + 1)
NI = P + 4 * GT + 1
NB = 2 * GT + 1
NEG = -1e30
EPS = 1e-5


def build(nc, x, ints, ee, w_proj, b_proj, attn, w_out, b_out, gamma, beta, out):
    table = nc.dram_tensor("table", (NPAD, ROW), F32, kind="Internal").ap()
    h_t_dram = nc.dram_tensor("h_t_dram", (D, NPAD), F32, kind="Internal").ap()

    with ExitStack() as ctx:
        def sb(name, shape, dt=F32):
            return ctx.enter_context(nc.sbuf_tensor(name, shape, dt))

        def sem(name):
            return ctx.enter_context(nc.semaphore(name))

        rows = sb("rows", [P, RING, GT, ROW])
        ee_sb = sb("ee_sb", [P, RING, GT // 2 * P])
        ints_sb = sb("ints_sb", [P, RING, NI], I32)
        acc = sb("acc", [P, 2, NPAD])
        x_sb = sb("x_sb", [P, NG * 4, D])
        h_ring = sb("h_ring", [P, 2, 4, D])
        ht_ring = sb("ht_ring", [P, 2, 4 * D])
        ident = sb("ident", [P, P])
        head_block = sb("head_block", [P, P])
        ones = sb("ones", [P, P])
        diag = sb("diag", [P, GT])
        iota_i = sb("iota_i", [P, WIN], I32)
        iota_f = sb("iota_f", [P, WIN])
        proj_sb = sb("proj_sb", [P, D + 2 * ED])
        wout_sb = sb("wout_sb", [P, D])
        rhs_set = sb("rhs_set", [P, ROW])
        b_col = sb("b_col", [P, 1])
        a_col = sb("a_col", [P, 1])
        b_rep = sb("b_rep", [P, P])
        w_node = sb("w_node", [P, ROW])
        w_edge = sb("w_edge", [P, ROW])
        bias_row = sb("bias_row", [P, ROW])
        w_out_t = sb("w_out_t", [P, D])
        bo_row = sb("bo_row", [P, D])
        ga_row = sb("ga_row", [P, D])
        be_row = sb("be_row", [P, D])
        eps_col = sb("eps_col", [P, 1])
        stats = sb("stats", [P, 2, 6])
        mean_var = sb("mean_var", [P, NG * 4, 2])
        mv4 = sb("mv4", [P, 4, 2])
        rstd = sb("rstd", [P, NG * 4])
        shift = sb("shift", [P, NG * 4])
        dst_s = sb("dst_s", [P, P])
        bnd_s = sb("bnd_s", [P, NB])
        new_seg = sb("new_seg", [P, P + 1])
        not_first = sb("not_first", [P, P])
        not_last = sb("not_last", [P, P])
        nb_masks = sb("nb_masks", [P, 3, NB])
        junk = sb("junk", [P, P])
        local = sb("local", [P, 2])
        spread = sb("spread", [P, NB])
        full = sb("full", [P, 3])
        decay_log = sb("decay_log", [P, 1])
        decay = sb("decay", [P, 1])
        fwd = sb("fwd", [P, P])
        seg_max = sb("seg_max", [P, P])
        spans = sb("spans", [1, Q], I32)
        span = sb("span", [1, RING], I32)
        dst_rel = sb("dst_rel", [P, GT])
        logit = sb("logit", [P, H, GT])
        centred = sb("centred", [P, H, GT])
        ex = sb("ex", [P, H, GT])
        one_hot = sb("one_hot", [P, GT, WIN])
        sx = sb("sx", [P, 2, QT, H, WIN])
        sx_sum = sb("sx_sum", [P, 2, H, WIN])
        rows_flat = rows[:, :, :, :].rearrange("p r t c -> p (r t c)")
        h_t_back = rows_flat[:, 0:NPAD]
        z_buf = rows_flat[:, NPAD:NPAD + 2 * 4 * P].rearrange("p (k c) -> p k c", k=2)
        res = acc[:, 1, :].rearrange("p (i c) -> p i c", c=D)
        h_t = acc[:, 0, :]
        table_sb = rows[:, :, :, :].rearrange("p r t c -> p (r t) c")

        ps_a = ctx.enter_context(nc.psum_tensor("ps_a", [P, 2, 2, 512], F32))
        ps_c = ctx.enter_context(nc.psum_tensor("ps_c", [P, 2, 512], F32))
        ps_b = ctx.enter_context(nc.psum_tensor("ps_b", [P, 512], F32))
        e_t = ps_b[:, 0:P]
        max_back = ps_b[:, P:2 * P]
        bounds_max = ps_b[:, 2 * P:2 * P + NB]

        w_loaded = sem("w_loaded")
        x_loaded = sem("x_loaded")
        consts_step = sem("consts_step")
        consts_done = sem("consts_done")
        set_step = sem("set_step")
        set_ready = sem("set_ready")
        set_mm = sem("set_mm")
        weights_done = sem("weights_done")
        st_done = sem("st_done")
        mv4_done = sem("mv4_done")
        mv_done = sem("mv_done")
        passed = sem("passed")
        passed_pool = sem("passed_pool")
        std_done = sem("std_done")
        rstd_step = sem("rstd_step")
        ln_done = sem("ln_done")
        h_done = sem("h_done")
        ht_psum = sem("ht_psum")
        ht_done = sem("ht_done")
        tb_psum = sem("tb_psum")
        tb_done = sem("tb_done")
        table_out = sem("table_out")
        ht_out = sem("ht_out")
        acc_zero = sem("acc_zero")
        ints_ready = [sem(f"ints_ready{r}") for r in range(RING)]
        ee_ready = [sem(f"ee_ready{r}") for r in range(RING)]
        gathered = [[sem(f"gathered{r}_{q}") for q in range(Q)] for r in range(RING)]
        pe_group = sem("pe_group")
        dve_group = sem("dve_group")
        projected = sem("projected")
        added = sem("added")
        packed = sem("packed")
        e_turned = sem("e_turned")
        scaled = sem("scaled")
        masked = sem("masked")
        local_done = sem("local_done")
        spread_done = sem("spread_done")
        bounds_done = sem("bounds_done")
        full_done = sem("full_done")
        decay_in = sem("decay_in")
        decay_done = sem("decay_done")
        fwd_done = sem("fwd_done")
        max_done = sem("max_done")
        max_turned = sem("max_turned")
        centred_done = sem("centred_done")
        ex_done = sem("ex_done")
        spans_done = sem("spans_done")
        span_done = sem("span_done")
        rel_done = sem("rel_done")
        hot_done = sem("hot_done")
        sx_done = sem("sx_done")
        sum_done = sem("sum_done")
        aggregated = sem("aggregated")
        drained = sem("drained")
        rescaled = sem("rescaled")
        x_rel = sem("x_rel")
        x_hot = sem("x_hot")
        x_sx = sem("x_sx")
        x_sum = sem("x_sum")
        x_agg = sem("x_agg")
        x_drained = sem("x_drained")
        ht_back = sem("ht_back")
        f_step = sem("f_step")
        z_done = sem("z_done")
        o_psum = sem("o_psum")
        o_bias = sem("o_bias")
        relu_done = sem("relu_done")
        f_st = sem("f_st")
        f_mv = sem("f_mv")
        f_std = sem("f_std")
        f_rstd = sem("f_rstd")
        normed = sem("normed")
        f_gamma = sem("f_gamma")
        f_beta = sem("f_beta")
        y_done = sem("y_done")
        y_out = sem("y_out")

        block = ctx.enter_context(nc.Block())

        def rounds(eng, body):
            with eng.Fori(0, LOOPS) as it:
                for r in range(RING):
                    body(it, r, False)
            for r in range(RING):
                body(LOOPS, r, r == RING - 1)

        def node_groups(eng, body):
            with eng.Fori(0, NG // 2) as it:
                for k in range(2):
                    body(it * 2 + k, k)
            body(NG - 1, 0)

        @block.sync
        def _(sp):
            sp.dma_start(proj_sb[:, 0:D + ED], w_proj).then_inc(w_loaded, 16)
            sp.dma_start(proj_sb[:, D + ED:D + 2 * ED], w_proj[:, D:D + ED]).then_inc(w_loaded, 16)
            sp.dma_start(wout_sb[:, :], w_out).then_inc(w_loaded, 16)
            sp.dma_start(b_col[:, :], b_proj.rearrange("(p a) -> p a", a=1)).then_inc(w_loaded, 16)
            sp.dma_start(a_col[:, :], attn.rearrange("h (d a) -> (h d) a", a=1)).then_inc(w_loaded, 16)
            sp.dma_start(bo_row[:, :], b_out.partition_broadcast(P)).then_inc(w_loaded, 16)
            sp.dma_start(ga_row[:, :], gamma.partition_broadcast(P)).then_inc(w_loaded, 16)
            sp.dma_start(be_row[:, :], beta.partition_broadcast(P)).then_inc(w_loaded, 16)

            def load(it, r, last):
                s = it * RING + r
                sp.wait_ge(pe_group, s + 1)
                sp.wait_ge(dve_group, s + 1)
                sp.dma_start(ints_sb[:, r, :], ints[bass.ds(s, 1)].rearrange("a p c -> (a p) c")).then_inc(ints_ready[r], 16)
                sp.dma_start(ee_sb[:, r, :], ee[bass.ds(s, 1)].rearrange("a p c -> (a p) c")).then_inc(ee_ready[r], 16)

            rounds(sp, load)
            sp.wait_ge(pe_group, NS - 1 + RING)
            sp.wait_ge(dve_group, NS - 1 + RING)
            sp.wait_ge(ht_out, 16)
            sp.dma_start(h_t_back, h_t_dram).then_inc(ht_back, 16)

        @block.gpsimd
        def _(pool):
            nc.gpsimd.memset(ident[:, :], 0.0).then_inc(consts_step, 1)
            nc.gpsimd.memset(head_block[:, :], 1.0).then_inc(consts_step, 1)
            nc.gpsimd.memset(ones[:, :], 1.0).then_inc(consts_done, 1)
            nc.gpsimd.memset(eps_col[:, :], EPS).then_inc(consts_done, 1)
            nc.gpsimd.iota(iota_i[:, :], [[1, WIN]], base=0, channel_multiplier=0).then_inc(consts_done, 1)
            nc.gpsimd.memset(new_seg[:, :], 0.0).then_inc(consts_done, 1)
            nc.gpsimd.memset(spread[:, :], 0.0).then_inc(consts_done, 1)
            pool.wait_ge(consts_step, 2)
            nc.gpsimd.affine_select(out=ident[:, :], in_=ident[:, :], compare_op=ALU.not_equal, fill=1.0, base=0,
                                    pattern=[[-1, P]], channel_multiplier=1).then_inc(consts_done, 1)
            hb = head_block[:, :].rearrange("p (h d) -> p h d", h=H)
            nc.gpsimd.affine_select(out=hb, in_=hb, compare_op=ALU.is_ge, fill=0.0, base=0,
                                    pattern=[[-HD, H], [0, HD]], channel_multiplier=1).then_inc(consts_step, 1)
            pool.wait_ge(consts_step, 3)
            nc.gpsimd.affine_select(out=hb, in_=hb, compare_op=ALU.is_ge, fill=0.0, base=HD - 1,
                                    pattern=[[HD, H], [0, HD]], channel_multiplier=-1).then_inc(consts_done, 1)

            def gather(it, r, last):
                s = it * RING + r
                pool.wait_ge(ints_ready[r], it * 16 + 16)
                pool.wait_ge(pe_group, s + 1)
                pool.sem_inc(passed_pool, 1)
                for q in range(Q):
                    for j in range(q * QT, q * QT + QT):
                        pool.indirect_dma_start(
                            out=rows[:, r, j, :], out_offset=None, in_=table,
                            in_offset=bass.IndirectOffsetOnAxis(
                                ap=ints_sb[:, r, P + GT + j:P + GT + j + 1], axis=0),
                        ).then_inc(gathered[r][q], 16)

            pool.wait_ge(table_out, 16 * NG)
            rounds(pool, gather)

            def finish(g, k):
                xs = x_sb[:, bass.ds(g * 4, 4), :]
                rs = res[:, bass.ds(g * 4, 4), :]
                row = [w[:, :].unsqueeze(1).to_broadcast([P, 4, D]) for w in (ga_row, be_row)]
                pool.wait_ge(normed, g * 4 + 4)
                pool.sem_inc(passed_pool, 1)
                nc.gpsimd.tensor_tensor(rs, rs, row[0], ALU.mult).then_inc(f_gamma, 1)
                nc.gpsimd.tensor_tensor(xs, xs, row[1], ALU.add).then_inc(f_beta, 1)
                pool.wait_ge(f_gamma, g + 1)
                pool.wait_ge(f_beta, g + 1)
                pool.sem_inc(passed_pool, 1)
                nc.gpsimd.tensor_tensor(xs, xs, rs, ALU.add).then_inc(y_done, 1)
            node_groups(pool, finish)

        @block.scalar
        def _(act):
            xr = x[:, :].rearrange("(i p) f -> p i f", p=P)
            act.dma_start(x_sb[:, :, :], xr).then_inc(x_loaded, 16)
            act.wait_ge(mv_done, NG)
            act.wait_ge(consts_done, 2)
            nc.scalar.activation(rstd[:, :], mean_var[:, :, 1], ACT.Sqrt, bias=eps_col[:, :]).then_inc(std_done, 1)
            act.wait_ge(ln_done, 1)

            def make_h(g, k):
                act.wait_ge(ht_psum, g + 1)
                for j in range(4):
                    i = g * 4 + j
                    last = nc.scalar.activation(h_ring[:, k, j, :], x_sb[:, bass.ds(i, 1), :].rearrange("p a f -> p (a f)"),
                                                ACT.Relu, bias=shift[:, bass.ds(i, 1)], scale=rstd[:, bass.ds(i, 1)])
                last.then_inc(h_done, 1)

            node_groups(act, make_h)

            def store_table(g, k):
                act.wait_ge(tb_done, g + 1)
                act.dma_start(table[bass.ds(g * 4 * P, 4 * P), :].rearrange("(j p) c -> p j c", p=P),
                              table_sb[:, bass.ds(g * 4, 4), :]).then_inc(table_out, 16)
            node_groups(act, store_table)
            act.wait_ge(ht_done, NG)
            act.dma_start(h_t_dram, h_t).then_inc(ht_out, 16)

            def exps(it, r, last):
                s = it * RING + r
                act.wait_ge(added, s * Q + Q)
                nc.scalar.copy(logit[:, :, :], rows[:, r, :, D:ROW].rearrange("p j h -> p h j")).then_inc(packed, 1)
                act.wait_ge(decay_in, s + 1)
                act.wait_ge(rescaled, s + 1)
                nc.scalar.activation(decay[:, :], decay_log[:, :], ACT.Exp).then_inc(decay_done, 1)
                act.wait_ge(centred_done, s + 1)
                act.wait_ge(sum_done, s * Q + 1)
                nc.scalar.activation(ex[:, :, :], centred[:, :, :], ACT.Exp).then_inc(ex_done, 1)

            rounds(act, exps)

            def relu(g, k):
                rs = res[:, bass.ds(g * 4, 4), :]
                act.wait_ge(o_bias, g + 1)
                nc.scalar.activation(rs, rs, ACT.Relu).then_inc(relu_done, 1)
            node_groups(act, relu)
            act.wait_ge(f_mv, NG)
            nc.scalar.activation(rstd[:, :], mean_var[:, :, 1], ACT.Sqrt, bias=eps_col[:, :]).then_inc(f_std, 1)
            act.wait_ge(f_rstd, 2)

            def normalise(g, k):
                for j in range(4):
                    i = g * 4 + j
                    r1 = res[:, bass.ds(i, 1), :].rearrange("p a f -> p (a f)")
                    nc.scalar.activation(r1, r1, ACT.Identity, bias=shift[:, bass.ds(i, 1)],
                                         scale=rstd[:, bass.ds(i, 1)]).then_inc(normed, 1)
            node_groups(act, normalise)
            full_rows = (NT - 1) * P
            act.wait_ge(y_done, NG)
            act.dma_start(out[0:full_rows, :].rearrange("(i p) f -> p i f", p=P),
                          x_sb[:, 0:NT - 1, :]).then_inc(y_out, 16)
            act.dma_start(out[full_rows:N, :], x_sb[0:N - full_rows, NT - 1, :]).then_inc(y_out, 16)
            act.wait_ge(y_out, 32)

        @block.tensor
        def _(pe):
            pe.sem_inc(pe_group, RING)
            pe.sem_inc(aggregated, 2)
            pe.sem_inc(ht_psum, 2)
            pe.wait_ge(set_ready, 3)
            nc.tensor.matmul(ps_a[:, 0, 0, 0:ROW], proj_sb[:, 0:D], rhs_set[:, :], start=True, stop=True).then_inc(set_mm, 1)
            nc.tensor.matmul(ps_a[:, 0, 1, 0:ROW], proj_sb[:, D:D + 2 * ED], rhs_set[:, :], start=True, stop=True).then_inc(set_mm, 1)
            nc.tensor.matmul(ps_a[:, 1, 0, 0:ROW], b_rep[:, :], rhs_set[:, :], start=True, stop=True).then_inc(set_mm, 1)
            nc.tensor.matmul(ps_a[:, 1, 1, 0:D], wout_sb[:, :], ident[:, :], start=True, stop=True).then_inc(set_mm, 1)
            pe.wait_ge(weights_done, 4)

            def turn_h(g, k):
                pe.wait_ge(h_done, g + 1)
                for j in range(4):
                    last = nc.tensor.transpose(ps_a[:, k, 0, j * P:(j + 1) * P], h_ring[:, k, j, :], ident[:, :])
                last.then_inc(ht_psum, 1)
                pe.wait_ge(ht_done, g + 1)
                for j in range(4):
                    last = nc.tensor.matmul(ps_c[:, j // 2, (j % 2) * ROW:(j % 2 + 1) * ROW],
                                            ht_ring[:, k, j * P:(j + 1) * P], w_node[:, :], start=True, stop=True)
                last.then_inc(tb_psum, 1)
                pe.wait_ge(tb_done, g + 1)
            node_groups(pe, turn_h)

            def project(n, q, r, it):
                if q == 0:
                    pe.wait_ge(ee_ready[r], it * 16 + 16)
                if not (isinstance(n, int) and n < 2):
                    pe.wait_ge(added, n - 1)
                half = (q * QT) // (GT // 2)
                for j in range(QT):
                    t = q * QT + j - half * (GT // 2)
                    last = nc.tensor.matmul(ps_a[:, q % 2, j // 2, (j % 2) * ROW:(j % 2 + 1) * ROW],
                                            ee_sb[half * ED:(half + 1) * ED, r, t * P:(t + 1) * P],
                                            w_edge[half * ED:(half + 1) * ED, :], start=True, stop=True)
                last.then_inc(projected, 1)

            for q in range(Q):
                project(q, q, 0, 0)

            passes = pe.alloc_register("pe_passes")
            pe.reg_mov(passes, 0)

            def group(it, r, last):
                s = it * RING + r
                r1 = (r + 1) % RING
                it1 = it + (r + 1) // RING
                pe.wait_ge(packed, s + 1)
                nc.tensor.transpose(e_t, logit[:, :, :].rearrange("p h j -> p (h j)"), ident[:, :]).then_inc(e_turned, 1)
                if not last:
                    project((s + 1) * Q, 0, r1, it1)
                pe.wait_ge(spread_done, s + 1)
                nc.tensor.matmul(bounds_max, head_block[:, :], spread[:, :], start=True, stop=True).then_inc(bounds_done, 1)
                if not last:
                    project((s + 1) * Q + 1, 1, r1, it1)
                pe.wait_ge(span_done, s + 1)
                pe.wait_ge(max_done, s + 1)
                nc.tensor.transpose(max_back, seg_max[:, :], ident[:, :]).then_inc(max_turned, 1)
                for q in range(Q):
                    n = s * Q + q
                    k = q % 2
                    pe.wait_ge(sum_done, n + 2)
                    pe.wait_ge(drained, n + 1)
                    window(r, q, k).then_inc(aggregated, 1)
                    if not last and q + 2 < Q:
                        project((s + 1) * Q + q + 2, q + 2, r1, it1)
                width = pe.value_load(span[0:1, r:r + 1], min_val=0, max_val=NPAD)
                with pe.If(width >= WIN):
                    with pe.Fori(WIN, width + 1, WIN):
                        done = pe.snap(passes, min_val=0, max_val=NS * NPAD)
                        for q in range(Q):
                            pe.wait_ge(x_sum, done * Q + q + 1)
                            window(r, q, q % 2).then_inc(x_agg, 1)
                        pe.reg_add(passes, passes, 1)
                pe.drain().then_inc(pe_group, 1)

            def window(r, q, k):
                for j in range(QT):
                    nc.tensor.matmul(ps_c[:, k, 0:H * WIN], rows[:, r, q * QT + j, 0:D],
                                     sx[:, k, j, :, :].rearrange("p h n -> p (h n)"), start=j == 0, stop=j == QT - 1)
                return nc.tensor.matmul(ps_c[:, k, H * WIN:2 * H * WIN], ones[:, :],
                                        sx_sum[:, k, :, :].rearrange("p h n -> p (h n)"), start=True, stop=True)

            rounds(pe, group)

            def out_proj(g, k):
                pe.wait_ge(z_done, g + 1)
                for j in range(4):
                    last = nc.tensor.matmul(ps_a[:, k, 0, j * P:(j + 1) * P], z_buf[:, k, j * P:(j + 1) * P],
                                            w_out_t[:, :], start=True, stop=True)
                last.then_inc(o_psum, 1)
            node_groups(pe, out_proj)

        @block.vector
        def _(dve):
            v = nc.vector

            def hold(what, value):
                dve.wait_ge(what, value)
                dve.sem_inc(passed, 1)

            dve.sem_inc(dve_group, RING)
            dve.sem_inc(drained, 2)
            dve.sem_inc(sum_done, 1)
            dve.sem_inc(rescaled, 1)
            dve.wait_ge(consts_done, 7)
            dve.wait_ge(w_loaded, 16 * 8)
            v.tensor_copy(iota_f[:, :], iota_i[:, :]).then_inc(set_step, 1)
            v.tensor_copy(rhs_set[:, 0:D], ident[:, :]).then_inc(set_ready, 1)
            v.tensor_scalar(rhs_set[:, D:ROW], head_block[:, :].rearrange("p (h d) -> p h d", h=H)[:, :, 0],
                            a_col[:, 0:1], None, ALU.mult).then_inc(set_ready, 1)
            v.tensor_scalar(b_rep[:, :], ones[:, :], b_col[:, 0:1], None, ALU.mult).then_inc(set_ready, 1)
            v.tensor_reduce(diag[:, :], ident[:, :].rearrange("p (h k) -> p k h", h=H), AX_X, ALU.add).then_inc(set_step, 1)
            dve.wait_ge(set_mm, 4)
            v.tensor_copy(w_node[:, :], ps_a[:, 0, 0, 0:ROW]).then_inc(weights_done, 1)
            v.tensor_copy(w_edge[:, :], ps_a[:, 0, 1, 0:ROW]).then_inc(weights_done, 1)
            v.tensor_copy(bias_row[:, :], ps_a[:, 1, 0, 0:ROW]).then_inc(weights_done, 1)
            v.tensor_copy(w_out_t[:, :], ps_a[:, 1, 1, 0:D]).then_inc(weights_done, 1)

            def moments(src, st, mv, mv4_base):
                def body(g, k):
                    for j in range(4):
                        i = g * 4 + j
                        v.bn_stats(stats[:, j % 2, :], src[:, bass.ds(i, 1), :].rearrange("p a f -> p (a f)")).then_inc(st, 1)
                        hold(st, i + 1)
                        v.bn_aggr(mv4[:, j, :], stats[:, j % 2, :]).then_inc(mv4_done, 1)
                    dve.wait_ge(mv4_done, mv4_base + g * 4 + 4)
                    v.tensor_copy(mean_var[:, bass.ds(g * 4, 4), :], mv4[:, :, :]).then_inc(mv, 1)
                return body

            dve.wait_ge(x_loaded, 16)
            node_groups(dve, moments(x_sb, st_done, mv_done, 0))
            dve.wait_ge(std_done, 1)
            v.reciprocal(rstd[:, :], rstd[:, :]).then_inc(rstd_step, 1)
            dve.wait_ge(rstd_step, 1)
            dve.wait_ge(mv_done, NG)
            v.scalar_tensor_tensor(out=shift[:, :], in0=mean_var[:, :, 0], scalar=-1.0, in1=rstd[:, :],
                                   op0=ALU.mult, op1=ALU.mult).then_inc(ln_done, 1)

            dve.wait_ge(weights_done, 4)

            def table_rows(g, k):
                dve.wait_ge(ht_psum, g + 3)
                v.tensor_copy(ht_ring[:, k, :], ps_a[:, k, 0, :])
                v.tensor_copy(h_t[:, bass.ds(g * 4 * P, 4 * P)], ps_a[:, k, 0, :]).then_inc(ht_done, 1)
                dve.wait_ge(tb_psum, g + 1)
                v.tensor_tensor(table_sb[:, bass.ds(g * 4, 4), :].rearrange("p (a b) c -> p a (b c)", a=2),
                                ps_c[:, :, 0:2 * ROW],
                                bias_row[:, :].unsqueeze(1).to_broadcast([P, 4, ROW]).rearrange("p (a b) c -> p a b c", a=2),
                                ALU.add).then_inc(tb_done, 1)
            node_groups(dve, table_rows)
            dve.wait_ge(ht_out, 16)
            v.memset(acc[:, :, :], 0.0).then_inc(acc_zero, 1)
            dve.wait_ge(acc_zero, 1)
            dve.wait_ge(set_step, 2)

            def add_rows(n, q, r, it):
                dve.wait_ge(projected, n + 1)
                dve.wait_ge(gathered[r][q], it * 16 * QT + 16 * QT)
                g = rows[:, r, q * QT:(q + 1) * QT, :].rearrange("p (a b) c -> p a (b c)", a=2)
                v.tensor_tensor(g, g, ps_a[:, q % 2, :, 0:2 * ROW], ALU.add).then_inc(added, 1)

            for q in range(Q):
                add_rows(q, q, 0, 0)

            passes = dve.alloc_register("dve_passes")
            dve.reg_mov(passes, 0)
            at = dve.alloc_register("extra_node")

            def make_hot(done):
                v.tensor_tensor(one_hot[:, :, :], iota_f[:, :].unsqueeze(1).to_broadcast([P, GT, WIN]),
                                dst_rel[:, :].unsqueeze(2).to_broadcast([P, GT, WIN]), ALU.is_equal).then_inc(done, 1)

            def make_sx(q, done):
                v.tensor_tensor(sx[:, q % 2, :, :, :],
                                one_hot[:, q * QT:(q + 1) * QT, :].unsqueeze(2).to_broadcast([P, QT, H, WIN]),
                                ex[:, :, q * QT:(q + 1) * QT].rearrange("p h t -> p t h").unsqueeze(3).to_broadcast([P, QT, H, WIN]),
                                ALU.mult).then_inc(done, 1)

            def sum_sx(q, done):
                v.tensor_reduce(sx_sum[:, q % 2, :, :], sx[:, q % 2, :, :, :].rearrange("p t h n -> p h n t"),
                                AX_X, ALU.add).then_inc(done, 1)

            def drain(q, node, done):
                for h in range(H):
                    mine = slice(h * HD, (h + 1) * HD)
                    a = acc[mine, :, bass.ds(node, WIN)]
                    last = v.tensor_tensor(a, a, ps_c[mine, q % 2, 0:2 * H * WIN].rearrange(
                        "p (a b) -> p a b", a=2)[:, :, h * WIN:(h + 1) * WIN], ALU.add)
                last.then_inc(done, 1)

            def group(it, r, last_group):
                s = it * RING + r
                r1 = (r + 1) % RING
                it1 = it + (r + 1) // RING
                iv = ints_sb[:, r, :]
                dve.wait_ge(ints_ready[r], it * 16 + 16)
                v.tensor_scalar(dst_s[:, :], iv[:, DST_ROWS], 1e30, None, ALU.mult).then_inc(scaled, 1)
                v.tensor_scalar(bnd_s[:, :], iv[:, BOUNDS], 1e30, None, ALU.mult).then_inc(scaled, 1)
                tile_bounds = iv[:, BOUNDS][:, 0:2 * GT].rearrange("p (q c) -> p q c", q=Q)
                v.tensor_tensor(spans[0:1, :], tile_bounds[0:1, :, 2 * QT - 1], tile_bounds[0:1, :, 0],
                                ALU.subtract).then_inc(spans_done, 1)
                v.tensor_tensor(dst_rel[:, :].rearrange("p (q t) -> p q t", q=Q),
                                iv[:, DST_COLS].rearrange("p (q t) -> p q t", q=Q),
                                tile_bounds[:, :, 0:1].to_broadcast([P, Q, QT]), ALU.subtract).then_inc(rel_done, 1)
                dve.wait_ge(scaled, s * 2 + 2)
                v.tensor_tensor(new_seg[:, 1:P], dst_s[:, 0:P - 1], dst_s[:, 1:P], ALU.subtract).then_inc(masked, 1)
                v.tensor_scalar(not_first[:, :], dst_s[:, :], dst_s[:, 0:1], NEG, ALU.not_equal, ALU.mult).then_inc(masked, 1)
                v.tensor_scalar(not_last[:, :], dst_s[:, :], dst_s[:, P - 1:P], NEG, ALU.not_equal, ALU.mult).then_inc(masked, 1)
                for m, node in enumerate((dst_s[:, 0:1], dst_s[:, P - 1:P], bnd_s[:, NB - 1:NB])):
                    v.tensor_scalar(nb_masks[:, m, :], bnd_s[:, :], node, NEG, ALU.not_equal, ALU.mult).then_inc(masked, 1)
                dve.wait_ge(spans_done, s + 1)
                v.tensor_reduce(span[:, r:r + 1], spans[:, :], AX_X, ALU.max).then_inc(span_done, 1)
                dve.wait_ge(span_done, s + 1)
                dve.wait_ge(rel_done, s + 1)
                make_hot(hot_done)
                dve.wait_ge(masked, s * 6 + 6)
                hold(e_turned, s + 1)
                for m, mask in enumerate((not_first, not_last)):
                    v.tensor_tensor_reduce(junk[:, :], e_t, mask[:, :], 1.0, 0.0, ALU.add, ALU.max, local[:, m:m + 1]).then_inc(local_done, 1)
                    hold(local_done, s * 2 + m + 1)
                v.tensor_tensor(spread[:, 0:2 * GT].rearrange("p (t m) -> p t m", m=2),
                                diag[:, :].unsqueeze(2).to_broadcast([P, GT, 2]),
                                local[:, :].unsqueeze(1).to_broadcast([P, GT, 2]), ALU.mult).then_inc(spread_done, 1)
                hold(bounds_done, s + 1)
                for m in range(3):
                    v.tensor_tensor_reduce(junk[:, 0:NB], bounds_max, nb_masks[:, m, :], 1.0, 0.0, ALU.add, ALU.max,
                                           full[:, m:m + 1]).then_inc(full_done, 1)
                    hold(full_done, s * 3 + m + 1)
                v.tensor_tensor(spread[:, NB - 1:NB], full[:, 1:2], diag[:, GT - 1:GT], ALU.mult)
                v.tensor_tensor(decay_log[:, :], bounds_max[:, NB - 1:NB], full[:, 2:3], ALU.subtract).then_inc(decay_in, 1)
                v.tensor_tensor_scan(fwd[:, :], new_seg[:, 0:P], e_t, full[:, 0:1], ALU.add, ALU.max).then_inc(fwd_done, 1)
                dve.wait_ge(fwd_done, s + 1)
                v.tensor_tensor_scan(seg_max[:, ::-1], new_seg[:, 1:P + 1][:, ::-1], fwd[:, ::-1], full[:, 1:2],
                                     ALU.add, ALU.max).then_inc(max_done, 1)
                node = dve.value_load(ints_sb[0:1, r, NI - 1:NI], min_val=0, max_val=LEAD_DST)
                dve.wait_ge(decay_done, s + 1)
                carried = acc[:, :, bass.ds(node, 1)]
                v.tensor_scalar(carried, carried, decay[:, 0:1], None, ALU.mult).then_inc(rescaled, 1)
                dve.wait_ge(max_turned, s + 1)
                v.tensor_tensor(centred[:, :, :], logit[:, :, :], max_back.rearrange("p (h j) -> p h j", h=H),
                                ALU.subtract).then_inc(centred_done, 1)
                if not last_group:
                    add_rows((s + 1) * Q, 0, r1, it1)
                dve.wait_ge(ex_done, s + 1)
                dve.wait_ge(hot_done, s + 1)
                for q in range(Q + 1):
                    n = s * Q + q
                    if q < Q:
                        dve.wait_ge(aggregated, n + 1)
                        make_sx(q, sx_done)
                        dve.wait_ge(sx_done, n + 1)
                        sum_sx(q, sum_done)
                    if q + 1 < Q and not last_group:
                        add_rows((s + 1) * Q + q + 1, q + 1, r1, it1)
                    if q > 0:
                        base = P + 2 * GT + (q - 1) * 2 * QT
                        node = dve.value_load(ints_sb[0:1, r, base:base + 1], min_val=0, max_val=PAD_DST)
                        dve.wait_ge(aggregated, n + 2)
                        dve.wait_ge(drained, n + 1)
                        if q == 1:
                            dve.wait_ge(rescaled, s + 2)
                        drain(q - 1, node, drained)
                width = dve.value_load(span[0:1, r:r + 1], min_val=0, max_val=NPAD)
                with dve.If(width >= WIN):
                    with dve.Fori(WIN, width + 1, WIN) as off:
                        done = dve.snap(passes, min_val=0, max_val=NS * NPAD)
                        dve.wait_ge(drained, s * Q + Q + 2)
                        v.tensor_scalar(dst_rel[:, :], dst_rel[:, :], -float(WIN), None, ALU.add).then_inc(x_rel, 1)
                        dve.wait_ge(x_rel, done + 1)
                        make_hot(x_hot)
                        dve.wait_ge(x_hot, done + 1)
                        for q in range(Q):
                            make_sx(q, x_sx)
                            dve.wait_ge(x_sx, done * Q + q + 1)
                            sum_sx(q, x_sum)
                            base = P + 2 * GT + q * 2 * QT
                            node = dve.value_load(ints_sb[0:1, r, base:base + 1], min_val=0, max_val=PAD_DST)
                            dve.wait_ge(x_agg, done * Q + q + 1)
                            dve.reg_alu(at, node + off, NPAD - WIN, ALU.min)
                            drain(q, dve.snap(at, min_val=0, max_val=NPAD - WIN), x_drained)
                            dve.wait_ge(x_drained, done * Q + q + 1)
                        dve.reg_add(passes, passes, 1)
                dve.drain().then_inc(dve_group, 1)

            rounds(dve, group)

            dve.wait_ge(drained, NS * Q + 2)
            dve.wait_ge(ht_back, 16)

            def make_z(g, k):
                cols = bass.ds(g * 4 * P, 4 * P)
                zk = z_buf[:, k, :]
                v.tensor_scalar(zk, acc[:, 1, cols], 1e-30, None, ALU.max).then_inc(f_step, 1)
                dve.wait_ge(f_step, g * 3 + 1)
                v.reciprocal(zk, zk).then_inc(f_step, 1)
                dve.wait_ge(f_step, g * 3 + 2)
                v.tensor_tensor(zk, zk, acc[:, 0, cols], ALU.mult).then_inc(f_step, 1)
                dve.wait_ge(f_step, g * 3 + 3)
                v.tensor_tensor(zk, zk, h_t_back[:, cols], ALU.add).then_inc(z_done, 1)
                dve.wait_ge(o_psum, g + 1)
                v.tensor_tensor(res[:, bass.ds(g * 4, 4), :], ps_a[:, k, 0, :].rearrange("p (j f) -> p j f", j=4),
                                bo_row[:, :].unsqueeze(1).to_broadcast([P, 4, D]), ALU.add).then_inc(o_bias, 1)
            node_groups(dve, make_z)
            dve.wait_ge(relu_done, NG)
            node_groups(dve, moments(res, f_st, f_mv, NG * 4))
            dve.wait_ge(f_std, 1)
            v.reciprocal(rstd[:, :], rstd[:, :]).then_inc(f_rstd, 1)
            dve.wait_ge(f_rstd, 1)
            dve.wait_ge(f_mv, NG)
            v.scalar_tensor_tensor(out=shift[:, :], in0=mean_var[:, :, 0], scalar=-1.0, in1=rstd[:, :],
                                   op0=ALU.mult, op1=ALU.mult).then_inc(f_rstd, 1)


def kernel(x, src, dst, edge_attr_64, L0_gnn_W_proj_w, L0_gnn_W_proj_b, L0_gnn_attn_vec, L0_gnn_W_out_w,
           L0_gnn_W_out_b, L0_gnn_ln_gamma, L0_gnn_ln_beta):
    import numpy as np
    import concourse.bacc as bacc
    from concourse.bass_utils import run_bass_kernel_spmd

    edges = NS * GT * P
    src, dst = np.asarray(src), np.asarray(dst)
    src_p = np.zeros(edges, src.dtype)
    src_p[:E] = src
    dst_p = np.full(edges, PAD_DST, dst.dtype)
    dst_p[:E] = dst
    src_t = src_p.reshape(NS, GT, P)
    dst_t = dst_p.reshape(NS, GT, P)
    before = np.concatenate([np.full(1, LEAD_DST, dst.dtype), dst_t[:-1, -1, -1]])
    bounds = np.concatenate([dst_t[:, :, [0, P - 1]].reshape(NS, 2 * GT), before[:, None]], axis=1)
    ints = np.concatenate([
        np.tile(dst_t, (1, H, 1)),
        dst_t.transpose(0, 2, 1),
        src_t.transpose(0, 2, 1),
        np.broadcast_to(bounds[:, None, :], (NS, P, NB)),
    ], axis=2)
    ee = np.asarray(edge_attr_64)
    ee_p = np.zeros((edges, ED), ee.dtype)
    ee_p[:E] = ee
    ee_t = ee_p.reshape(NS, 2, GT // 2 * P, ED).transpose(0, 1, 3, 2).reshape(NS, P, GT // 2 * P)
    x = np.asarray(x)
    x_p = np.zeros((NPAD, D), x.dtype)
    x_p[:N] = x
    arrays = {
        "x_in": x_p, "ints_in": ints, "ee_in": ee_t, "w_proj_in": L0_gnn_W_proj_w, "b_proj_in": L0_gnn_W_proj_b,
        "attn_in": L0_gnn_attn_vec, "w_out_in": L0_gnn_W_out_w, "b_out_in": L0_gnn_W_out_b,
        "gamma_in": L0_gnn_ln_gamma, "beta_in": L0_gnn_ln_beta,
    }
    arrays = {k: np.ascontiguousarray(a) for k, a in arrays.items()}
    nc = bacc.Bacc("TRN2", target_bir_lowering=False, num_devices=1)
    args = [nc.dram_tensor(k, a.shape, mybir.dt.from_np(a.dtype), kind="ExternalInput").ap() for k, a in arrays.items()]
    out = nc.dram_tensor("out", (N, D), F32, kind="ExternalOutput").ap()
    build(nc, *args, out)
    return run_bass_kernel_spmd(nc, [arrays], core_ids=[0]).results[0]["out"]
```

```python
from contextlib import ExitStack

import concourse.bass as bass
from concourse import mybir

F32 = mybir.dt.float32
I32 = mybir.dt.int32
ALU = mybir.AluOpType
ACT = mybir.ActivationFunctionType
AX_X = mybir.AxisListType.X

P = 128
N, E, D, ED = 6250, 206250, 128, 64
H, HD = 4, 32
ROW = D + H
GT = 32
Q = 8
QT = GT // Q
WIN = 20
RING = 3
NT = -(-N // P)
NG = -(-NT // 4)
NPAD = NG * 4 * P
TILES = -(-E // P)
NS = -(-TILES // GT)
assert NS % RING == 0 and H * GT == P and Q * QT == GT and NG % 2 == 1
LOOPS = NS // RING - 1
Q_LAST = -(-(TILES - (NS - 1) * GT) // QT)
PAD_DST = N
LEAD_DST = N + 1
DST_ROWS = slice(0, P)
DST_COLS = slice(P, P + GT)
SRC_COLS = slice(P + GT, P + 2 * GT)
BOUNDS = slice(P + 2 * GT, P + 4 * GT + 1)
NI = P + 4 * GT + 1
NB = 2 * GT + 1
NEG = -1e30
EPS = 1e-5
BF16 = mybir.dt.bfloat16


def build(nc, x, ints, ee, w_proj, b_proj, attn, w_out, b_out, gamma, beta, out):
    table = nc.dram_tensor("table", (NPAD, ROW), F32, kind="Internal").ap()
    o_dram = nc.dram_tensor("o_dram", (P, NPAD), F32, kind="Internal").ap()

    with ExitStack() as ctx:
        def sb(name, shape, dt=F32):
            return ctx.enter_context(nc.sbuf_tensor(name, shape, dt))

        def sem(name):
            return ctx.enter_context(nc.semaphore(name))

        rows = sb("rows", [P, RING, GT, ROW])
        ee_sb = sb("ee_sb", [P, RING, GT // 2 * P])
        ints_sb = sb("ints_sb", [P, RING, NI], I32)
        acc = sb("acc", [P, 2, NPAD])
        x_sb = sb("x_sb", [P, NG * 4, D])
        h_ring = sb("h_ring", [P, 2, 4, D])
        ht_ring = sb("ht_ring", [P, 2, 4 * D])
        ident = sb("ident", [P, P])
        head_block = sb("head_block", [P, P])
        ones = sb("ones", [P, P])
        head_pick = sb("head_pick", [P, 2 * H * (NG - 1) + H])
        diag = sb("diag", [P, GT])
        iota_i = sb("iota_i", [P, WIN], I32)
        iota_f = sb("iota_f", [P, WIN])
        proj_sb = sb("proj_sb", [P, D + 2 * ED])
        wout_sb = sb("wout_sb", [P, D])
        rhs_set = sb("rhs_set", [P, ROW])
        b_col = sb("b_col", [P, 1])
        a_col = sb("a_col", [P, 1])
        b_rep = sb("b_rep", [P, P])
        w_node = sb("w_node", [P, ROW])
        w_edge = sb("w_edge", [P, ROW])
        bias_row = sb("bias_row", [P, ROW])
        w_out_t = sb("w_out_t", [P, D])
        bo_row = sb("bo_row", [P, D])
        ga_row = sb("ga_row", [P, D])
        be_row = sb("be_row", [P, D])
        eps_col = sb("eps_col", [P, 1])
        stats = sb("stats", [P, 2, 6])
        mv4 = sb("mv4", [P, 2, 4, 2])
        std4 = sb("std4", [P, 2, 4])
        rstd = sb("rstd", [P, NG * 4])
        shift = sb("shift", [P, NG * 4])
        dst_s = sb("dst_s", [P, P])
        bnd_s = sb("bnd_s", [P, NB])
        new_seg = sb("new_seg", [P, P + 1])
        not_first = sb("not_first", [P, P])
        not_last = sb("not_last", [P, P])
        nb_masks = sb("nb_masks", [P, 3, NB])
        junk_bounds = sb("junk_bounds", [P, 3, NB])
        junk = sb("junk", [P, 2, P])
        local = sb("local", [P, 2])
        spread = sb("spread", [P, NB])
        full = sb("full", [P, 3])
        decay_log = sb("decay_log", [P, 1])
        decay = sb("decay", [P, 1])
        fwd = sb("fwd", [P, P])
        seg_max = sb("seg_max", [P, P])
        spans = sb("spans", [1, Q], I32)
        span = sb("span", [1, RING], I32)
        dst_rel = sb("dst_rel", [P, RING, GT])
        logit = sb("logit", [P, H, GT])
        centred = sb("centred", [P, H, GT])
        ex = sb("ex", [P, H, GT])
        one_hot = sb("one_hot", [P, RING, GT, WIN], BF16)
        sx = sb("sx", [P, 2, QT, H, WIN])
        sx_sum = sb("sx_sum", [P, 2, H, WIN])
        rows_flat = rows[:, :, :, :].rearrange("p r t c -> p (r t c)")
        o_back = rows_flat[:, 0:NPAD]
        z_buf = rows_flat[:, NPAD:NPAD + 2 * 4 * P].rearrange("p (k c) -> p k c", k=2)
        recip = rows_flat[0:H * NG, NPAD + 2 * 4 * P:NPAD + 3 * 4 * P]
        back_sel = ee_sb[0:H * NG, 0, 0:NG * P]
        o_sb = rows_flat[:, RING * GT * ROW - NPAD:RING * GT * ROW]
        res = acc[:, 1, :].rearrange("p (i c) -> p i c", c=D)
        h_t = acc[:, 0, :]
        table_sb = rows[:, :, :, :].rearrange("p r t c -> p (r t) c")

        ps_a = ctx.enter_context(nc.psum_tensor("ps_a", [P, 2, 2, 512], F32))
        ps_c = ctx.enter_context(nc.psum_tensor("ps_c", [P, 2, 512], F32))
        ps_d = ctx.enter_context(nc.psum_tensor("ps_d", [P, 512], F32))
        ps_b = ctx.enter_context(nc.psum_tensor("ps_b", [P, 512], F32))
        e_t = ps_b[:, 0:P]
        max_back = ps_b[:, P:2 * P]
        bounds_max = ps_b[:, 2 * P:2 * P + NB]

        w_loaded = sem("w_loaded")
        x_first = sem("x_first")
        x_rest = sem("x_rest")
        x_beta = sem("x_beta")
        consts_step = sem("consts_step")
        consts_done = sem("consts_done")
        set_step = sem("set_step")
        set_ready = sem("set_ready")
        set_mm = sem("set_mm")
        weights_done = sem("weights_done")
        stats_done = sem("stats_done")
        mv4_done = sem("mv4_done")
        passed = sem("passed")
        passed_pool = sem("passed_pool")
        std_done = sem("std_done")
        rstd_step = sem("rstd_step")
        ln_done = sem("ln_done")
        h_done = sem("h_done")
        ht_psum = sem("ht_psum")
        ht_done = sem("ht_done")
        ht_kept = sem("ht_kept")
        tb_psum = sem("tb_psum")
        tb_done = sem("tb_done")
        table_out = sem("table_out")
        ht_again = sem("ht_again")
        o_pre_psum = sem("o_pre_psum")
        o_pre = sem("o_pre")
        o_out = sem("o_out")
        acc_zero = sem("acc_zero")
        ints_ready = [sem(f"ints_ready{r}") for r in range(RING)]
        ee_ready = [sem(f"ee_ready{r}") for r in range(RING)]
        gathered = [[sem(f"gathered{r}_{q}") for q in range(Q)] for r in range(RING)]
        pe_group = sem("pe_group")
        dve_group = sem("dve_group")
        projected = sem("projected")
        added = sem("added")
        packed = sem("packed")
        e_turned = sem("e_turned")
        scaled = sem("scaled")
        masked = sem("masked")
        local_done = sem("local_done")
        spread_done = sem("spread_done")
        bounds_done = sem("bounds_done")
        full_done = sem("full_done")
        carry_done = sem("carry_done")
        decay_in = sem("decay_in")
        decay_done = sem("decay_done")
        fwd_done = sem("fwd_done")
        max_done = sem("max_done")
        max_turned = sem("max_turned")
        centred_done = sem("centred_done")
        ex_done = sem("ex_done")
        spans_done = sem("spans_done")
        span_done = sem("span_done")
        rel_done = sem("rel_done")
        hot_done = sem("hot_done")
        sx_done = sem("sx_done")
        sum_done = sem("sum_done")
        aggregated = sem("aggregated")
        drained = sem("drained")
        rescaled = sem("rescaled")
        x_rel = sem("x_rel")
        x_hot = sem("x_hot")
        x_sx = sem("x_sx")
        x_sum = sem("x_sum")
        x_agg = sem("x_agg")
        x_drained = sem("x_drained")
        o_again = sem("o_again")
        sel_zero = sem("sel_zero")
        sel_done = sem("sel_done")
        den_psum = sem("den_psum")
        den_safe = sem("den_safe")
        recip_done = sem("recip_done")
        rec_psum = sem("rec_psum")
        z_done = sem("z_done")
        o_psum = sem("o_psum")
        o_added = sem("o_added")
        relu_done = sem("relu_done")
        f_stats = sem("f_stats")
        f_mv4 = sem("f_mv4")
        f_std = sem("f_std")
        f_rstd = sem("f_rstd")
        f_ln = sem("f_ln")
        normed = sem("normed")
        f_gamma = sem("f_gamma")
        y_done = sem("y_done")
        y_out = sem("y_out")

        block = ctx.enter_context(nc.Block())

        def rounds(eng, body):
            with eng.Fori(0, LOOPS) as it:
                for r in range(RING):
                    body(it, r, Q, Q)
            body(LOOPS, 0, Q, Q)
            body(LOOPS, 1, Q, Q_LAST)
            body(LOOPS, 2, Q_LAST, 0)

        def node_groups(eng, step, lag=0, after_two=None):
            for g in range(2):
                step(g, g)
            if after_two is not None:
                after_two()
            with eng.Fori(1, NG // 2) as it:
                for k in range(2):
                    step(it * 2 + k, k)
            for g in range(NG - 1, NG + lag):
                step(g, g % 2)

        def there(g):
            return not isinstance(g, int) or 0 <= g < NG

        def table_psum(k):
            return ps_a[:, k, :, 0:2 * ROW]

        def turn_psum(k):
            return ps_b if k else ps_d

        def tile(a, i):
            return a[:, bass.ds(i, 1), :].rearrange("p a f -> p (a f)")

        @block.sync
        def _(sp):
            xr = x[:, :].rearrange("(i p) f -> p i f", p=P)
            sp.dma_start(x_sb[:, 0:8, :], xr[:, 0:8, :]).then_inc(x_first, 16)
            sp.dma_start(x_sb[:, 8:NG * 4, :], xr[:, 8:NG * 4, :]).then_inc(x_rest, 16)
            def load(it, r, windows, after):
                s = it * RING + r
                sp.wait_ge(pe_group, s + 1)
                sp.wait_ge(dve_group, s + 1)
                sp.dma_start(ints_sb[:, r, :], ints[bass.ds(s, 1)].rearrange("a p c -> (a p) c")).then_inc(ints_ready[r], 16)
                sp.dma_start(ee_sb[:, r, :], ee[bass.ds(s, 1)].rearrange("a p c -> (a p) c")).then_inc(ee_ready[r], 16)

            def store_table(g, k):
                sp.wait_ge(tb_done, g + 1)
                sp.dma_start(table[bass.ds(g * 4 * P, 4 * P), :].rearrange("(j p) c -> p j c", p=P),
                             table_sb[:, bass.ds(g * 4, 4), :]).then_inc(table_out, 16)
            node_groups(sp, store_table)
            rounds(sp, load)
            sp.wait_ge(pe_group, NS - 1 + RING)
            sp.wait_ge(dve_group, NS - 1 + RING)
            sp.wait_ge(o_out, 16)
            sp.dma_start(o_back, o_dram).then_inc(o_again, 16)

            def store_out(g, k):
                sp.wait_ge(y_done, g + 1)
                if isinstance(g, int) and g == NG - 1:
                    first = g * 4 * P
                    sp.dma_start(out[first:N, :], x_sb[0:N - first, g * 4, :]).then_inc(y_out, 16)
                else:
                    sp.dma_start(out[bass.ds(g * 4 * P, 4 * P), :].rearrange("(i p) f -> p i f", p=P),
                                 x_sb[:, bass.ds(g * 4, 4), :]).then_inc(y_out, 16)
            node_groups(sp, store_out)
            sp.wait_ge(y_out, 16 * NG)

        @block.gpsimd
        def _(pool):
            nc.gpsimd.memset(ident[:, :], 0.0).then_inc(consts_step, 1)
            nc.gpsimd.memset(head_block[:, :], 1.0).then_inc(consts_step, 1)
            nc.gpsimd.memset(ones[:, :], 1.0).then_inc(consts_done, 1)
            nc.gpsimd.memset(eps_col[:, :], EPS).then_inc(consts_done, 1)
            nc.gpsimd.iota(iota_i[:, :], [[1, WIN]], base=0, channel_multiplier=0).then_inc(consts_done, 1)
            nc.gpsimd.memset(new_seg[:, :], 0.0).then_inc(consts_done, 1)
            nc.gpsimd.memset(spread[:, :], 0.0).then_inc(consts_done, 1)
            nc.gpsimd.memset(head_pick[:, :], 0.0).then_inc(consts_step, 1)
            pool.wait_ge(consts_step, 3)
            nc.gpsimd.affine_select(out=ident[:, :], in_=ident[:, :], compare_op=ALU.not_equal, fill=1.0, base=0,
                                    pattern=[[-1, P]], channel_multiplier=1).then_inc(consts_done, 1)
            hb = head_block[:, :].rearrange("p (h d) -> p h d", h=H)
            nc.gpsimd.affine_select(out=hb, in_=hb, compare_op=ALU.is_ge, fill=0.0, base=0,
                                    pattern=[[-HD, H], [0, HD]], channel_multiplier=1).then_inc(consts_step, 1)
            mid = head_pick[:, H * (NG - 1):H * NG]
            nc.gpsimd.affine_select(out=mid, in_=mid, compare_op=ALU.not_equal, fill=1.0, base=0,
                                    pattern=[[-HD, H]], channel_multiplier=1).then_inc(consts_done, 1)
            pool.wait_ge(consts_step, 4)
            nc.gpsimd.affine_select(out=hb, in_=hb, compare_op=ALU.is_ge, fill=0.0, base=HD - 1,
                                    pattern=[[HD, H], [0, HD]], channel_multiplier=-1).then_inc(consts_done, 1)

            def gather(it, r, windows, after):
                s = it * RING + r
                pool.wait_ge(ints_ready[r], it * 16 + 16)
                pool.wait_ge(pe_group, s + 1)
                if r > 0:
                    pool.wait_ge(o_out, 16)
                pool.sem_inc(passed_pool, 1)
                for q in range(windows):
                    for j in range(q * QT, q * QT + QT):
                        pool.indirect_dma_start(
                            out=rows[:, r, j, :], out_offset=None, in_=table,
                            in_offset=bass.IndirectOffsetOnAxis(
                                ap=ints_sb[:, r, P + GT + j:P + GT + j + 1], axis=0),
                        ).then_inc(gathered[r][q], 16)

            pool.wait_ge(table_out, 16 * NG)
            rounds(pool, gather)

            pool.wait_ge(pe_group, NS - 1 + RING)
            nc.gpsimd.memset(back_sel, 0.0).then_inc(sel_zero, 1)
            pool.wait_ge(sel_zero, 1)
            bs = back_sel.rearrange("m (g f) -> m g f", g=NG)
            for h in range(H):
                nc.gpsimd.affine_select(out=bs[:, :, h * HD:(h + 1) * HD], in_=bs[:, :, h * HD:(h + 1) * HD],
                                        compare_op=ALU.not_equal, fill=1.0, base=-h,
                                        pattern=[[-H, NG], [0, HD]], channel_multiplier=1).then_inc(sel_done, 1)

            def finish(g, k):
                xs = x_sb[:, bass.ds(g * 4, 4), :]
                rs = res[:, bass.ds(g * 4, 4), :]
                pool.wait_ge(normed, g + 1)
                pool.sem_inc(passed_pool, 1)
                nc.gpsimd.tensor_tensor(rs, rs, ga_row[:, :].unsqueeze(1).to_broadcast([P, 4, D]),
                                        ALU.mult).then_inc(f_gamma, 1)
                pool.wait_ge(f_gamma, g + 1)
                pool.sem_inc(passed_pool, 1)
                nc.gpsimd.tensor_tensor(xs, xs, rs, ALU.add).then_inc(y_done, 1)
            node_groups(pool, finish)

        @block.scalar
        def _(act):
            act.dma_start(proj_sb[:, 0:D + ED], w_proj).then_inc(w_loaded, 16)
            act.dma_start(proj_sb[:, D + ED:D + 2 * ED], w_proj[:, D:D + ED]).then_inc(w_loaded, 16)
            act.dma_start(wout_sb[:, :], w_out).then_inc(w_loaded, 16)
            act.dma_start(b_col[:, :], b_proj.rearrange("(p a) -> p a", a=1)).then_inc(w_loaded, 16)
            act.dma_start(a_col[:, :], attn.rearrange("h (d a) -> (h d) a", a=1)).then_inc(w_loaded, 16)
            act.dma_start(bo_row[:, :], b_out.partition_broadcast(P)).then_inc(w_loaded, 16)
            act.dma_start(ga_row[:, :], gamma.partition_broadcast(P)).then_inc(w_loaded, 16)
            act.dma_start(be_row[:, :], beta.partition_broadcast(P)).then_inc(w_loaded, 16)
            act.wait_ge(consts_done, 2)

            def node_part(g, k):
                if there(g):
                    act.wait_ge(mv4_done, g * 4 + 4)
                    nc.scalar.activation(std4[:, k, :], mv4[:, k, :, 1], ACT.Sqrt, bias=eps_col[:, :]).then_inc(std_done, 1)
                    act.wait_ge(ln_done, g + 1)
                    if not (isinstance(g, int) and g < 2):
                        act.wait_ge(ht_psum, g - 1)
                    for j in range(4):
                        i = g * 4 + j
                        last = nc.scalar.activation(h_ring[:, k, j, :], tile(x_sb, i), ACT.Relu,
                                                    bias=shift[:, bass.ds(i, 1)], scale=rstd[:, bass.ds(i, 1)])
                    last.then_inc(h_done, 1)
                if there(g - 1):
                    act.wait_ge(ht_done, g)
                    nc.scalar.copy(h_t[:, bass.ds((g - 1) * 4 * P, 4 * P)], ht_ring[:, 1 - k, :]).then_inc(ht_kept, 1)
            node_groups(act, node_part, lag=1)
            act.wait_ge(tb_psum, NG)

            def bring_back(g, k):
                act.wait_ge(ht_kept, NG)
                if not (isinstance(g, int) and g < 2):
                    act.wait_ge(o_pre_psum, g - 1)
                nc.scalar.copy(ht_ring[:, k, :], h_t[:, bass.ds(g * 4 * P, 4 * P)]).then_inc(ht_again, 1)
            node_groups(act, bring_back)
            act.wait_ge(o_pre, NG)
            act.dma_start(o_dram, o_sb).then_inc(o_out, 16)

            def pack_group(s, r, windows):
                act.wait_ge(added, s * Q + windows)
                nc.scalar.copy(logit[:, :, :], rows[:, r, :, D:ROW].rearrange("p j h -> p h j")).then_inc(packed, 1)

            pack_group(0, 0, Q)

            def exps(it, r, windows, after):
                s = it * RING + r
                act.wait_ge(decay_in, s + 1)
                act.wait_ge(rescaled, s + 1)
                nc.scalar.activation(decay[:, :], decay_log[:, :], ACT.Exp).then_inc(decay_done, 1)
                act.wait_ge(centred_done, s + 1)
                act.wait_ge(sum_done, s * Q + 1)
                nc.scalar.activation(ex[:, :, :], centred[:, :, :], ACT.Exp).then_inc(ex_done, 1)
                if after:
                    pack_group(s + 1, (r + 1) % RING, after)

            rounds(act, exps)

            def final_part(g, k):
                if there(g - 2):
                    act.wait_ge(f_mv4, (g - 2) * 4 + 4)
                    nc.scalar.activation(std4[:, k, :], mv4[:, k, :, 1], ACT.Sqrt, bias=eps_col[:, :]).then_inc(f_std, 1)
                if there(g - 1):
                    rs = res[:, bass.ds((g - 1) * 4, 4), :]
                    act.wait_ge(o_added, g)
                    nc.scalar.activation(rs, rs, ACT.Relu).then_inc(relu_done, 1)
                if there(g - 2):
                    act.wait_ge(f_ln, g - 1)
                    for j in range(4):
                        i = (g - 2) * 4 + j
                        last = nc.scalar.activation(tile(res, i), tile(res, i), ACT.Identity,
                                                    bias=shift[:, bass.ds(i, 1)], scale=rstd[:, bass.ds(i, 1)])
                    last.then_inc(normed, 1)
            node_groups(act, final_part, lag=2)

        @block.tensor
        def _(pe):
            pe.sem_inc(pe_group, RING)
            pe.sem_inc(aggregated, 2)
            pe.wait_ge(set_ready, 3)
            nc.tensor.matmul(ps_a[:, 0, 0, 0:ROW], proj_sb[:, 0:D], rhs_set[:, :], start=True, stop=True).then_inc(set_mm, 1)
            nc.tensor.matmul(ps_a[:, 0, 1, 0:ROW], proj_sb[:, D:D + 2 * ED], rhs_set[:, :], start=True, stop=True).then_inc(set_mm, 1)
            nc.tensor.matmul(ps_a[:, 1, 0, 0:ROW], b_rep[:, :], rhs_set[:, :], start=True, stop=True).then_inc(set_mm, 1)
            nc.tensor.matmul(ps_a[:, 1, 1, 0:D], wout_sb[:, :], ident[:, :], start=True, stop=True).then_inc(set_mm, 1)
            pe.wait_ge(weights_done, 4)

            def node_part(g, k):
                if there(g):
                    pe.wait_ge(h_done, g + 1)
                    if not (isinstance(g, int) and g < 2):
                        pe.wait_ge(ht_done, g - 1)
                    for j in range(4):
                        last = nc.tensor.transpose(turn_psum(k)[:, j * P:(j + 1) * P], h_ring[:, k, j, :], ident[:, :])
                    last.then_inc(ht_psum, 1)
                if there(g - 1):
                    pe.wait_ge(ht_done, g)
                    if not (isinstance(g, int) and g < 3):
                        pe.wait_ge(tb_done, g - 2)
                    for j in range(4):
                        last = nc.tensor.matmul(table_psum(1 - k)[:, j // 2, (j % 2) * ROW:(j % 2 + 1) * ROW],
                                                ht_ring[:, 1 - k, j * P:(j + 1) * P], w_node[:, :], start=True, stop=True)
                    last.then_inc(tb_psum, 1)
            node_groups(pe, node_part, lag=1)

            def pre_output(g, k):
                pe.wait_ge(ht_again, g + 1)
                if not (isinstance(g, int) and g < 2):
                    pe.wait_ge(o_pre, g - 1)
                for j in range(4):
                    last = nc.tensor.matmul(ps_c[:, k, j * P:(j + 1) * P], ht_ring[:, k, j * P:(j + 1) * P],
                                            w_out_t[:, :], start=True, stop=True)
                last.then_inc(o_pre_psum, 1)
            node_groups(pe, pre_output)
            pe.wait_ge(o_pre, NG)
            pe.wait_ge(tb_done, NG)

            def project(n, q, r, it):
                if q == 0:
                    pe.wait_ge(ee_ready[r], it * 16 + 16)
                if not (isinstance(n, int) and n < 2):
                    pe.wait_ge(added, n - 1)
                for j in (0, 2, 1, 3):
                    half = j // 2
                    t = q * 2 + j % 2
                    last = nc.tensor.matmul(ps_a[:, q % 2, half, (j % 2) * ROW:(j % 2 + 1) * ROW],
                                            ee_sb[half * ED:(half + 1) * ED, r, t * P:(t + 1) * P],
                                            w_edge[half * ED:(half + 1) * ED, :], start=True, stop=True)
                last.then_inc(projected, 1)

            for q in range(Q):
                project(q, q, 0, 0)

            passes = pe.alloc_register("pe_passes")
            pe.reg_mov(passes, 0)

            def turn_logits(s):
                pe.wait_ge(packed, s + 1)
                nc.tensor.transpose(e_t, logit[:, :, :].rearrange("p h j -> p (h j)"), ident[:, :]).then_inc(e_turned, 1)

            turn_logits(0)

            def group(it, r, windows, after):
                s = it * RING + r
                r1 = (r + 1) % RING
                it1 = it + (r + 1) // RING
                pe.wait_ge(spread_done, s + 1)
                nc.tensor.matmul(bounds_max, head_block[:, :], spread[:, :], start=True, stop=True).then_inc(bounds_done, 1)
                for q in range(min(2, after)):
                    project((s + 1) * Q + q, q, r1, it1)
                pe.wait_ge(span_done, s + 1)
                pe.wait_ge(max_done, s + 1)
                nc.tensor.transpose(max_back, seg_max[:, :], ident[:, :]).then_inc(max_turned, 1)
                for q in range(windows):
                    n = s * Q + q
                    k = q % 2
                    if q == windows - 1 and after:
                        turn_logits(s + 1)
                    pe.wait_ge(sum_done, n + 2)
                    pe.wait_ge(drained, n + 1)
                    window(r, q, k).then_inc(aggregated, 1)
                    if q + 2 < after:
                        project((s + 1) * Q + q + 2, q + 2, r1, it1)
                width = pe.value_load(span[0:1, r:r + 1], min_val=0, max_val=NPAD)
                with pe.If(width >= WIN):
                    with pe.Fori(WIN, width + 1, WIN):
                        done = pe.snap(passes, min_val=0, max_val=NS * NPAD)
                        for q in range(Q):
                            pe.wait_ge(x_sum, done * Q + q + 1)
                            window(r, q, q % 2).then_inc(x_agg, 1)
                        pe.reg_add(passes, passes, 1)
                pe.drain().then_inc(pe_group, 1)

            def window(r, q, k):
                for j in range(QT):
                    nc.tensor.matmul(ps_c[:, k, 0:H * WIN], rows[:, r, q * QT + j, 0:D],
                                     sx[:, k, j, :, :].rearrange("p h n -> p (h n)"), start=j == 0, stop=j == QT - 1)
                return nc.tensor.matmul(ps_c[:, k, H * WIN:2 * H * WIN], ones[:, :],
                                        sx_sum[:, k, :, :].rearrange("p h n -> p (h n)"), start=True, stop=True)

            rounds(pe, group)

            pe.wait_ge(drained, (NS - 1) * Q + Q_LAST + 2)
            pe.wait_ge(dve_group, NS + RING)
            for g in range(NG):
                first = H * (NG - 1 - g)
                last = nc.tensor.matmul(ps_d[0:H * NG, :], head_pick[:, first:first + H * NG],
                                        acc[:, 1, g * 4 * P:(g + 1) * 4 * P], start=g == 0, stop=g == NG - 1)
            last.then_inc(den_psum, 1)
            pe.wait_ge(recip_done, 1)
            pe.wait_ge(sel_done, H)

            def recip_back(g):
                nc.tensor.matmul(ps_a[:, g % 2, 1, :], back_sel[:, g * P:(g + 1) * P], recip,
                                 start=True, stop=True).then_inc(rec_psum, 1)
            for g in range(NG + 1):
                if g < NG:
                    if g >= 2:
                        pe.wait_ge(z_done, g - 1)
                    recip_back(g)
                if g >= 1:
                    k = (g - 1) % 2
                    pe.wait_ge(z_done, g)
                    if g >= 3:
                        pe.wait_ge(o_added, g - 2)
                    for j in range(4):
                        last = nc.tensor.matmul(ps_a[:, k, 0, j * P:(j + 1) * P], z_buf[:, k, j * P:(j + 1) * P],
                                                w_out_t[:, :], start=True, stop=True)
                    last.then_inc(o_psum, 1)

        @block.vector
        def _(dve):
            v = nc.vector

            def hold(what, value):
                dve.wait_ge(what, value)
                dve.sem_inc(passed, 1)

            dve.sem_inc(dve_group, RING)
            dve.sem_inc(drained, 2)
            dve.sem_inc(sum_done, 1)
            dve.sem_inc(rescaled, 1)
            dve.wait_ge(consts_done, 8)
            dve.wait_ge(w_loaded, 16 * 8)
            v.tensor_copy(iota_f[:, :], iota_i[:, :]).then_inc(set_step, 1)
            v.tensor_copy(rhs_set[:, 0:D], ident[:, :]).then_inc(set_ready, 1)
            v.tensor_scalar(rhs_set[:, D:ROW], head_block[:, :].rearrange("p (h d) -> p h d", h=H)[:, :, 0],
                            a_col[:, 0:1], None, ALU.mult).then_inc(set_ready, 1)
            v.tensor_scalar(b_rep[:, :], ones[:, :], b_col[:, 0:1], None, ALU.mult).then_inc(set_ready, 1)
            v.tensor_reduce(diag[:, :], ident[:, :].rearrange("p (h k) -> p k h", h=H), AX_X, ALU.add).then_inc(set_step, 1)
            dve.wait_ge(set_mm, 4)
            v.tensor_copy(w_node[:, :], ps_a[:, 0, 0, 0:ROW]).then_inc(weights_done, 1)
            v.tensor_copy(w_edge[:, :], ps_a[:, 0, 1, 0:ROW]).then_inc(weights_done, 1)
            v.tensor_copy(bias_row[:, :], ps_a[:, 1, 0, 0:ROW]).then_inc(weights_done, 1)
            v.tensor_copy(w_out_t[:, :], ps_a[:, 1, 1, 0:D]).then_inc(weights_done, 1)

            def moments(src, g, k, stats_sem, mv_sem):
                for j in range(4):
                    i = g * 4 + j
                    v.bn_stats(stats[:, j % 2, :], tile(src, i)).then_inc(stats_sem, 1)
                    hold(stats_sem, i + 1)
                    v.bn_aggr(mv4[:, k, j, :], stats[:, j % 2, :]).then_inc(mv_sem, 1)

            def scale_shift(g, k, std_sem, rstd_sem, ln_sem):
                dve.wait_ge(std_sem, g + 1)
                v.reciprocal(rstd[:, bass.ds(g * 4, 4)], std4[:, k, :]).then_inc(rstd_sem, 1)
                dve.wait_ge(rstd_sem, g + 1)
                v.scalar_tensor_tensor(out=shift[:, bass.ds(g * 4, 4)], in0=mv4[:, k, :, 0], scalar=-1.0,
                                       in1=rstd[:, bass.ds(g * 4, 4)], op0=ALU.mult, op1=ALU.mult).then_inc(ln_sem, 1)

            def node_part(g, k):
                if there(g):
                    moments(x_sb, g, k, stats_done, mv4_done)
                if there(g - 1):
                    if not (isinstance(g, int) and g < 3):
                        dve.wait_ge(ht_kept, g - 2)
                    dve.wait_ge(ht_psum, g)
                    v.tensor_copy(ht_ring[:, 1 - k, :], turn_psum(1 - k)[:, :]).then_inc(ht_done, 1)
                if there(g):
                    scale_shift(g, k, std_done, rstd_step, ln_done)
                if there(g - 2):
                    dve.wait_ge(tb_psum, g - 1)
                    v.tensor_tensor(table_sb[:, bass.ds((g - 2) * 4, 4), :].rearrange("p (a b) c -> p a (b c)", a=2),
                                    table_psum(k),
                                    bias_row[:, :].unsqueeze(1).to_broadcast([P, 4, ROW]).rearrange("p (a b) c -> p a b c", a=2),
                                    ALU.add).then_inc(tb_done, 1)
            dve.wait_ge(x_first, 16)
            hold(weights_done, 4)
            node_groups(dve, node_part, lag=2, after_two=lambda: dve.wait_ge(x_rest, 16))

            def pre_output(g, k):
                dve.wait_ge(o_pre_psum, g + 1)
                v.tensor_tensor(o_sb[:, bass.ds(g * 4 * P, 4 * P)].rearrange("p (j f) -> p j f", j=4),
                                ps_c[:, k, :].rearrange("p (j f) -> p j f", j=4),
                                bo_row[:, :].unsqueeze(1).to_broadcast([P, 4, D]), ALU.add).then_inc(o_pre, 1)
            dve.wait_ge(table_out, 16 * NG)
            node_groups(dve, pre_output)
            dve.wait_ge(ht_again, NG)
            v.memset(acc[:, :, :], 0.0).then_inc(acc_zero, 1)
            v.tensor_tensor(x_sb[:, :, :], x_sb[:, :, :], be_row[:, :].unsqueeze(1).to_broadcast([P, NG * 4, D]),
                            ALU.add).then_inc(x_beta, 1)
            dve.wait_ge(acc_zero, 1)
            dve.wait_ge(set_step, 2)

            def add_rows(n, q, r, it):
                dve.wait_ge(projected, n + 1)
                dve.wait_ge(gathered[r][q], it * 16 * QT + 16 * QT)
                g = rows[:, r, q * QT:(q + 1) * QT, :].rearrange("p (a b) c -> p a (b c)", a=2)
                v.tensor_tensor(g, g, ps_a[:, q % 2, :, 0:2 * ROW], ALU.add).then_inc(added, 1)

            for q in range(Q):
                add_rows(q, q, 0, 0)

            passes = dve.alloc_register("dve_passes")
            dve.reg_mov(passes, 0)
            at = dve.alloc_register("extra_node")

            def make_hot(r, done):
                v.tensor_tensor(one_hot[:, r, :, :], iota_f[:, :].unsqueeze(1).to_broadcast([P, GT, WIN]),
                                dst_rel[:, r, :].unsqueeze(2).to_broadcast([P, GT, WIN]), ALU.is_equal).then_inc(done, 1)

            def make_sx(r, q, done):
                v.tensor_tensor(sx[:, q % 2, :, :, :],
                                one_hot[:, r, q * QT:(q + 1) * QT, :].unsqueeze(2).to_broadcast([P, QT, H, WIN]),
                                ex[:, :, q * QT:(q + 1) * QT].rearrange("p h t -> p t h").unsqueeze(3).to_broadcast([P, QT, H, WIN]),
                                ALU.mult).then_inc(done, 1)

            def sum_sx(q, done):
                v.tensor_reduce(sx_sum[:, q % 2, :, :], sx[:, q % 2, :, :, :].rearrange("p t h n -> p h n t"),
                                AX_X, ALU.add).then_inc(done, 1)

            def drain(q, node, done):
                for h in range(H):
                    mine = slice(h * HD, (h + 1) * HD)
                    a = acc[mine, :, bass.ds(node, WIN)]
                    last = v.tensor_tensor(a, a, ps_c[mine, q % 2, 0:2 * H * WIN].rearrange(
                        "p (a b) -> p a b", a=2)[:, :, h * WIN:(h + 1) * WIN], ALU.add)
                last.then_inc(done, 1)

            def prepare(s, it, r, windows):
                iv = ints_sb[:, r, :]
                dve.wait_ge(ints_ready[r], it * 16 + 16)
                v.tensor_scalar(dst_s[:, :], iv[:, DST_ROWS], 1e30, None, ALU.mult).then_inc(scaled, 1)
                v.tensor_scalar(bnd_s[:, :], iv[:, BOUNDS], 1e30, None, ALU.mult).then_inc(scaled, 1)
                tile_bounds = iv[:, BOUNDS][:, 0:2 * GT].rearrange("p (q c) -> p q c", q=Q)
                v.tensor_tensor(spans[0:1, :], tile_bounds[0:1, :, 2 * QT - 1], tile_bounds[0:1, :, 0],
                                ALU.subtract).then_inc(spans_done, 1)
                v.tensor_tensor(dst_rel[:, r, :].rearrange("p (q t) -> p q t", q=Q),
                                iv[:, DST_COLS].rearrange("p (q t) -> p q t", q=Q),
                                tile_bounds[:, :, 0:1].to_broadcast([P, Q, QT]), ALU.subtract).then_inc(rel_done, 1)
                dve.wait_ge(scaled, s * 2 + 2)
                v.tensor_tensor(new_seg[:, 1:P], dst_s[:, 0:P - 1], dst_s[:, 1:P], ALU.subtract).then_inc(masked, 1)
                v.tensor_scalar(not_first[:, :], dst_s[:, :], dst_s[:, 0:1], NEG, ALU.not_equal, ALU.mult).then_inc(masked, 1)
                v.tensor_scalar(not_last[:, :], dst_s[:, :], dst_s[:, P - 1:P], NEG, ALU.not_equal, ALU.mult).then_inc(masked, 1)
                for m, node in enumerate((dst_s[:, 0:1], dst_s[:, P - 1:P], bnd_s[:, NB - 1:NB])):
                    v.tensor_scalar(nb_masks[:, m, :], bnd_s[:, :], node, NEG, ALU.not_equal, ALU.mult).then_inc(masked, 1)
                dve.wait_ge(spans_done, s + 1)
                v.tensor_reduce(span[:, r:r + 1], spans[:, :], AX_X, ALU.max).then_inc(span_done, 1)
                dve.wait_ge(span_done, s + 1)
                dve.wait_ge(rel_done, s + 1)
                make_hot(r, hot_done)

            def local_maxima(s):
                dve.wait_ge(masked, s * 6 + 6)
                hold(e_turned, s + 1)
                for m, mask in enumerate((not_first, not_last)):
                    v.tensor_tensor_reduce(junk[:, m, :], e_t, mask[:, :], 1.0, 0.0, ALU.add, ALU.max,
                                           local[:, m:m + 1]).then_inc(local_done, 1)
                dve.wait_ge(local_done, s * 2 + 2)
                v.tensor_tensor(spread[:, 0:2 * GT].rearrange("p (t m) -> p t m", m=2),
                                diag[:, :].unsqueeze(2).to_broadcast([P, GT, 2]),
                                local[:, :].unsqueeze(1).to_broadcast([P, GT, 2]), ALU.mult).then_inc(spread_done, 1)

            prepare(0, 0, 0, Q)
            local_maxima(0)

            def group(it, r, windows, after):
                s = it * RING + r
                r1 = (r + 1) % RING
                it1 = it + (r + 1) // RING
                hold(bounds_done, s + 1)
                for m in range(3):
                    v.tensor_tensor_reduce(junk_bounds[:, m, :], bounds_max, nb_masks[:, m, :], 1.0, 0.0, ALU.add, ALU.max,
                                           full[:, m:m + 1]).then_inc(full_done, 1)
                hold(full_done, s * 3 + 3)
                v.tensor_tensor_scan(fwd[:, :], new_seg[:, 0:P], e_t, full[:, 0:1], ALU.add, ALU.max).then_inc(fwd_done, 1)
                v.tensor_tensor(spread[:, NB - 1:NB], full[:, 1:2], diag[:, GT - 1:GT], ALU.mult).then_inc(carry_done, 1)
                v.tensor_tensor(decay_log[:, :], bounds_max[:, NB - 1:NB], full[:, 2:3], ALU.subtract).then_inc(decay_in, 1)
                dve.wait_ge(fwd_done, s + 1)
                v.tensor_tensor_scan(seg_max[:, ::-1], new_seg[:, 1:P + 1][:, ::-1], fwd[:, ::-1], full[:, 1:2],
                                     ALU.add, ALU.max).then_inc(max_done, 1)
                node = dve.value_load(ints_sb[0:1, r, NI - 1:NI], min_val=0, max_val=LEAD_DST)
                dve.wait_ge(decay_done, s + 1)
                carried = acc[:, :, bass.ds(node, 1)]
                v.tensor_scalar(carried, carried, decay[:, 0:1], None, ALU.mult).then_inc(rescaled, 1)
                dve.wait_ge(max_turned, s + 1)
                v.tensor_tensor(centred[:, :, :], logit[:, :, :], max_back.rearrange("p (h j) -> p h j", h=H),
                                ALU.subtract).then_inc(centred_done, 1)
                if after:
                    add_rows((s + 1) * Q, 0, r1, it1)
                dve.wait_ge(ex_done, s + 1)
                dve.wait_ge(hot_done, s + 1)
                for q in range(windows + 1):
                    n = s * Q + q
                    if q < windows:
                        dve.wait_ge(aggregated, n + 1)
                        make_sx(r, q, sx_done)
                        dve.wait_ge(sx_done, n + 1)
                        sum_sx(q, sum_done)
                    if q + 1 < after:
                        add_rows((s + 1) * Q + q + 1, q + 1, r1, it1)
                    if q == 2 and after:
                        prepare(s + 1, it1, r1, after)
                    if q == windows and after:
                        local_maxima(s + 1)
                    if q > 0:
                        base = P + 2 * GT + (q - 1) * 2 * QT
                        node = dve.value_load(ints_sb[0:1, r, base:base + 1], min_val=0, max_val=PAD_DST)
                        dve.wait_ge(aggregated, n + 2)
                        dve.wait_ge(drained, n + 1)
                        if q == 1:
                            dve.wait_ge(rescaled, s + 2)
                        drain(q - 1, node, drained)
                width = dve.value_load(span[0:1, r:r + 1], min_val=0, max_val=NPAD)
                with dve.If(width >= WIN):
                    with dve.Fori(WIN, width + 1, WIN) as off:
                        done = dve.snap(passes, min_val=0, max_val=NS * NPAD)
                        dve.wait_ge(drained, s * Q + windows + 2)
                        v.tensor_scalar(dst_rel[:, r, :], dst_rel[:, r, :], -float(WIN), None, ALU.add).then_inc(x_rel, 1)
                        dve.wait_ge(x_rel, done + 1)
                        make_hot(r, x_hot)
                        dve.wait_ge(x_hot, done + 1)
                        for q in range(Q):
                            make_sx(r, q, x_sx)
                            dve.wait_ge(x_sx, done * Q + q + 1)
                            sum_sx(q, x_sum)
                            base = P + 2 * GT + q * 2 * QT
                            node = dve.value_load(ints_sb[0:1, r, base:base + 1], min_val=0, max_val=PAD_DST)
                            dve.wait_ge(x_agg, done * Q + q + 1)
                            dve.reg_alu(at, node + off, NPAD - WIN, ALU.min)
                            drain(q, dve.snap(at, min_val=0, max_val=NPAD - WIN), x_drained)
                            dve.wait_ge(x_drained, done * Q + q + 1)
                        dve.reg_add(passes, passes, 1)
                dve.drain().then_inc(dve_group, 1)

            rounds(dve, group)

            dve.wait_ge(den_psum, 1)
            v.tensor_scalar(recip, ps_d[0:H * NG, :], 1e-30, None, ALU.max).then_inc(den_safe, 1)
            dve.wait_ge(den_safe, 1)
            v.reciprocal(recip, recip).then_inc(recip_done, 1)
            dve.wait_ge(o_again, 16)
            dve.wait_ge(x_beta, 1)

            def final_part(g, k):
                if there(g - 2):
                    hold(relu_done, g - 1)
                    moments(res, g - 2, k, f_stats, f_mv4)
                if there(g):
                    cols = bass.ds(g * 4 * P, 4 * P)
                    dve.wait_ge(rec_psum, g + 1)
                    if not (isinstance(g, int) and g < 2):
                        dve.wait_ge(o_psum, g - 1)
                    v.tensor_tensor(z_buf[:, k, :], acc[:, 0, cols], ps_a[:, k, 1, :], ALU.mult).then_inc(z_done, 1)
                if there(g - 1):
                    dve.wait_ge(o_psum, g)
                    v.tensor_tensor(res[:, bass.ds((g - 1) * 4, 4), :], ps_a[:, 1 - k, 0, :].rearrange("p (j f) -> p j f", j=4),
                                    o_back[:, bass.ds((g - 1) * 4 * P, 4 * P)].rearrange("p (j f) -> p j f", j=4),
                                    ALU.add).then_inc(o_added, 1)
                if there(g - 2):
                    scale_shift(g - 2, k, f_std, f_rstd, f_ln)
            node_groups(dve, final_part, lag=2)


def kernel(x, src, dst, edge_attr_64, L0_gnn_W_proj_w, L0_gnn_W_proj_b, L0_gnn_attn_vec, L0_gnn_W_out_w,
           L0_gnn_W_out_b, L0_gnn_ln_gamma, L0_gnn_ln_beta):
    import numpy as np
    import concourse.bacc as bacc
    from concourse.bass_utils import run_bass_kernel_spmd

    edges = NS * GT * P
    src, dst = np.asarray(src), np.asarray(dst)
    src_p = np.zeros(edges, src.dtype)
    src_p[:E] = src
    dst_p = np.full(edges, PAD_DST, dst.dtype)
    dst_p[:E] = dst
    src_t = src_p.reshape(NS, GT, P)
    dst_t = dst_p.reshape(NS, GT, P)
    before = np.concatenate([np.full(1, LEAD_DST, dst.dtype), dst_t[:-1, -1, -1]])
    bounds = np.concatenate([dst_t[:, :, [0, P - 1]].reshape(NS, 2 * GT), before[:, None]], axis=1)
    ints = np.concatenate([
        np.tile(dst_t, (1, H, 1)),
        dst_t.transpose(0, 2, 1),
        src_t.transpose(0, 2, 1),
        np.broadcast_to(bounds[:, None, :], (NS, P, NB)),
    ], axis=2)
    ee = np.asarray(edge_attr_64)
    ee_p = np.zeros((edges, ED), ee.dtype)
    ee_p[:E] = ee
    ee_t = ee_p.reshape(NS, Q, 2, QT // 2 * P, ED).transpose(0, 2, 4, 1, 3).reshape(NS, P, GT // 2 * P)
    x = np.asarray(x)
    x_p = np.zeros((NPAD, D), x.dtype)
    x_p[:N] = x
    arrays = {
        "x_in": x_p, "ints_in": ints, "ee_in": ee_t, "w_proj_in": L0_gnn_W_proj_w, "b_proj_in": L0_gnn_W_proj_b,
        "attn_in": L0_gnn_attn_vec, "w_out_in": L0_gnn_W_out_w, "b_out_in": L0_gnn_W_out_b,
        "gamma_in": L0_gnn_ln_gamma, "beta_in": L0_gnn_ln_beta,
    }
    arrays = {k: np.ascontiguousarray(a) for k, a in arrays.items()}
    nc = bacc.Bacc("TRN2", target_bir_lowering=False, num_devices=1)
    args = [nc.dram_tensor(k, a.shape, mybir.dt.from_np(a.dtype), kind="ExternalInput").ap() for k, a in arrays.items()]
    out = nc.dram_tensor("out", (N, D), F32, kind="ExternalOutput").ap()
    build(nc, *args, out)
    return run_bass_kernel_spmd(nc, [arrays], core_ids=[0]).results[0]["out"]
```

```python
from contextlib import ExitStack

import concourse.bass as bass
from concourse import mybir

F32 = mybir.dt.float32
I32 = mybir.dt.int32
ALU = mybir.AluOpType
ACT = mybir.ActivationFunctionType
AX_X = mybir.AxisListType.X

P = 128
N, E, D, ED = 6250, 206250, 128, 64
H, HD = 4, 32
ROW = D + H
GT = 32
Q = 8
QT = GT // Q
WIN = 20
RING = 3
NT = -(-N // P)
NG = -(-NT // 4)
NPAD = NG * 4 * P
DC = 2 * P
CH = NPAD // DC
TILES = -(-E // P)
NS = -(-TILES // GT)
assert NS % RING == 0 and H * GT == P and Q * QT == GT and NG % 2 == 1
LOOPS = NS // RING - 1
Q_LAST = -(-(TILES - (NS - 1) * GT) // QT)
PAD_DST = N
LEAD_DST = N + 1
DST_ROWS = slice(0, P)
DST_COLS = slice(P, P + GT)
SRC_COLS = slice(P + GT, P + 2 * GT)
BOUNDS = slice(P + 2 * GT, P + 4 * GT + 1)
NI = P + 4 * GT + 1
NB = 2 * GT + 1
NEG = -1e30
EPS = 1e-5
BF16 = mybir.dt.bfloat16


def build(nc, x, ints, ee, w_proj, b_proj, attn, w_out, b_out, gamma, beta, out):
    table = nc.dram_tensor("table", (NT * P, ROW), F32, kind="Internal").ap()
    o_dram = nc.dram_tensor("o_dram", (P, NT * P), F32, kind="Internal").ap()

    with ExitStack() as ctx:
        def sb(name, shape, dt=F32):
            return ctx.enter_context(nc.sbuf_tensor(name, shape, dt))

        def sem(name):
            return ctx.enter_context(nc.semaphore(name))

        rows = sb("rows", [P, RING, GT, ROW])
        ee_sb = sb("ee_sb", [P, RING, GT // 2 * P])
        ints_sb = sb("ints_sb", [P, RING, NI], I32)
        acc = sb("acc", [P, 2, NPAD])
        x_sb = sb("x_sb", [P, NT, D])
        h_ring = sb("h_ring", [P, 2, 4, D])
        ht_ring = sb("ht_ring", [P, 2, 4 * D])
        ident = sb("ident", [P, P])
        head_block = sb("head_block", [P, P])
        ones = sb("ones", [P, P])
        diag = sb("diag", [P, GT])
        iota_i = sb("iota_i", [P, WIN], I32)
        iota_f = sb("iota_f", [P, WIN])
        proj_sb = sb("proj_sb", [P, D + 2 * ED])
        wout_sb = sb("wout_sb", [P, D])
        rhs_set = sb("rhs_set", [P, ROW])
        b_col = sb("b_col", [P, 1])
        a_col = sb("a_col", [P, 1])
        b_rep = sb("b_rep", [P, P])
        w_node = sb("w_node", [P, ROW])
        w_edge = sb("w_edge", [P, ROW])
        bias_row = sb("bias_row", [P, ROW])
        w_out_t = sb("w_out_t", [P, D])
        bo_row = sb("bo_row", [P, D])
        ga_row = sb("ga_row", [P, D])
        be_row = sb("be_row", [P, D])
        eps_col = sb("eps_col", [P, 1])
        stats = sb("stats", [P, 2, 4, 6])
        mv4 = sb("mv4", [P, 2, 4, 2])
        std4 = sb("std4", [P, 2, 4])
        rstd = sb("rstd", [P, NG * 4])
        shift = sb("shift", [P, NG * 4])
        dst_s = sb("dst_s", [P, P])
        bnd_s = sb("bnd_s", [P, NB])
        new_seg = sb("new_seg", [P, P + 1])
        not_first = sb("not_first", [P, P])
        not_last = sb("not_last", [P, P])
        nb_masks = sb("nb_masks", [P, 3, NB])
        junk_bounds = sb("junk_bounds", [P, 3, NB])
        junk = sb("junk", [P, 2, P])
        local = sb("local", [P, 2])
        spread = sb("spread", [P, NB])
        full = sb("full", [P, 3])
        decay_log = sb("decay_log", [P, 1])
        decay = sb("decay", [P, 1])
        fwd = sb("fwd", [P, P])
        seg_max = sb("seg_max", [P, P])
        spans = sb("spans", [1, Q], I32)
        span = sb("span", [1, RING], I32)
        dst_rel = sb("dst_rel", [P, RING, GT])
        logit = sb("logit", [P, H, GT])
        centred = sb("centred", [P, H, GT])
        ex = sb("ex", [P, RING, H, GT])
        one_hot = sb("one_hot", [P, RING, GT, WIN], BF16)
        sx = sb("sx", [P, 4, QT, H, WIN])
        sx_sum = sb("sx_sum", [P, 2, 2, H, WIN])
        rows_flat = rows[:, :, :, :].rearrange("p r t c -> p (r t c)")
        o_back = rows_flat[:, 0:NT * P]
        z_buf = rows_flat[:, NPAD:NPAD + 2 * 4 * P].rearrange("p (k c) -> p k c", k=2)
        recip = rows_flat[0:H * CH, 2 * GT * ROW:2 * GT * ROW + DC]
        back_sel = ee_sb[:, :, :].rearrange("p r c -> p (r c)")[0:H * CH, 0:CH * P]
        o_sb = rows_flat[:, RING * GT * ROW - NT * P:RING * GT * ROW]
        res = acc[:, 1, :].rearrange("p (i c) -> p i c", c=D)
        h_t = acc[:, 0, :]
        table_sb = rows[:, :, :, :].rearrange("p r t c -> p (r t) c")

        ps_a = ctx.enter_context(nc.psum_tensor("ps_a", [P, 2, 2, 512], F32))
        ps_c = ctx.enter_context(nc.psum_tensor("ps_c", [P, 2, 512], F32))
        ps_d = ctx.enter_context(nc.psum_tensor("ps_d", [P, 512], F32))
        ps_b = ctx.enter_context(nc.psum_tensor("ps_b", [P, 512], F32))
        e_t = ps_b[:, 0:P]
        max_back = ps_b[:, P:2 * P]
        bounds_max = ps_b[:, 2 * P:2 * P + NB]

        w_loaded = sem("w_loaded")
        x_first = sem("x_first")
        x_middle = sem("x_middle")
        x_rest = sem("x_rest")
        x_beta = sem("x_beta")
        consts_step = sem("consts_step")
        consts_done = sem("consts_done")
        set_step = sem("set_step")
        set_ready = sem("set_ready")
        set_mm = sem("set_mm")
        weights_done = sem("weights_done")
        stats_done = sem("stats_done")
        mv4_done = sem("mv4_done")
        passed = sem("passed")
        passed_pool = sem("passed_pool")
        std_done = sem("std_done")
        rstd_step = sem("rstd_step")
        ln_done = sem("ln_done")
        h_done = sem("h_done")
        ht_psum = sem("ht_psum")
        ht_done = sem("ht_done")
        ht_kept = sem("ht_kept")
        tb_psum = sem("tb_psum")
        tb_done = sem("tb_done")
        table_out = sem("table_out")
        ht_again = sem("ht_again")
        o_pre_psum = sem("o_pre_psum")
        o_pre = sem("o_pre")
        o_out = sem("o_out")
        acc_zero = sem("acc_zero")
        ints_ready = [sem(f"ints_ready{r}") for r in range(RING)]
        ee_ready = [sem(f"ee_ready{r}") for r in range(RING)]
        gathered = [[sem(f"gathered{r}_{q}") for q in range(Q)] for r in range(RING)]
        pe_group = sem("pe_group")
        dve_group = sem("dve_group")
        projected = sem("projected")
        added = sem("added")
        packed = sem("packed")
        e_turned = sem("e_turned")
        scaled = sem("scaled")
        masked = sem("masked")
        local_done = sem("local_done")
        spread_done = sem("spread_done")
        bounds_done = sem("bounds_done")
        full_done = sem("full_done")
        carry_done = sem("carry_done")
        decay_in = sem("decay_in")
        decay_done = sem("decay_done")
        fwd_done = sem("fwd_done")
        max_done = sem("max_done")
        max_turned = sem("max_turned")
        centred_done = sem("centred_done")
        ex_done = sem("ex_done")
        spans_done = sem("spans_done")
        span_done = sem("span_done")
        rel_done = sem("rel_done")
        hot_done = sem("hot_done")
        sx_done = sem("sx_done")
        sum_done = sem("sum_done")
        pair_done = sem("pair_done")
        in_acc = sem("in_acc")
        rescaled = sem("rescaled")
        x_rel = sem("x_rel")
        x_hot = sem("x_hot")
        x_sx = sem("x_sx")
        x_sum = sem("x_sum")
        x_agg = sem("x_agg")
        x_drained = sem("x_drained")
        o_again = sem("o_again")
        sel_zero = sem("sel_zero")
        sel_done = sem("sel_done")
        den_rows = sem("den_rows")
        den_safe = sem("den_safe")
        recip_done = sem("recip_done")
        rec_psum = sem("rec_psum")
        z_done = sem("z_done")
        o_psum = sem("o_psum")
        o_added = sem("o_added")
        relu_done = sem("relu_done")
        f_stats = sem("f_stats")
        f_mv4 = sem("f_mv4")
        f_std = sem("f_std")
        f_rstd = sem("f_rstd")
        f_ln = sem("f_ln")
        normed = sem("normed")
        f_gamma = sem("f_gamma")
        y_done = sem("y_done")
        y_out = sem("y_out")

        block = ctx.enter_context(nc.Block())

        def rounds(eng, body):
            with eng.Fori(0, LOOPS) as it:
                for r in range(RING):
                    body(it, r, Q, Q, Q)
            body(LOOPS, 0, Q, Q, Q_LAST)
            body(LOOPS, 1, Q, Q_LAST, 0)
            body(LOOPS, 2, Q_LAST, 0, 0)

        def node_groups(eng, step, lag=0, before={}):
            first = 4 if lag else 2
            for g in range(first):
                if g in before:
                    before[g]()
                step(g, g % 2)
            if first in before:
                before[first]()
            with eng.Fori(first // 2, NG // 2) as it:
                for k in range(2):
                    step(it * 2 + k, k)
            for g in range(NG - 1, NG + lag):
                step(g, g % 2)

        def tiles_of(g):
            return NT - (NG - 1) * 4 if isinstance(g, int) and g == NG - 1 else 4

        def there(g):
            return not isinstance(g, int) or 0 <= g < NG

        def table_psum(k):
            return ps_a[:, k, :, 0:2 * ROW]

        def turn_psum(k):
            return ps_b if k else ps_d

        def tile(a, i):
            return a[:, bass.ds(i, 1), :].rearrange("p a f -> p (a f)")

        xr = x[:, :].rearrange("(i p) f -> p i f", p=P)

        @block.sync
        def _(sp):
            sp.dma_start(x_sb[:, 0:8, :], xr[:, 0:8, :]).then_inc(x_first, 16)
            sp.dma_start(bo_row[:, :], b_out.partition_broadcast(P)).then_inc(w_loaded, 16)
            sp.dma_start(ga_row[:, :], gamma.partition_broadcast(P)).then_inc(w_loaded, 16)
            sp.dma_start(be_row[:, :], beta.partition_broadcast(P)).then_inc(w_loaded, 16)

            def load(it, r, windows, after, after2):
                s = it * RING + r
                sp.wait_ge(pe_group, s + 1)
                sp.wait_ge(dve_group, s + 1)
                sp.dma_start(ints_sb[:, r, :], ints[bass.ds(s, 1)].rearrange("a p c -> (a p) c")).then_inc(ints_ready[r], 16)
                sp.dma_start(ee_sb[:, r, :], ee[bass.ds(s, 1)].rearrange("a p c -> (a p) c")).then_inc(ee_ready[r], 16)

            def store_table(g, k):
                sp.wait_ge(tb_done, g + 1)
                t = tiles_of(g)
                sp.dma_start(table[bass.ds(g * 4 * P, t * P), :].rearrange("(j p) c -> p j c", p=P),
                             table_sb[:, bass.ds(g * 4, t), :]).then_inc(table_out, 16)
            node_groups(sp, store_table)
            rounds(sp, load)
            sp.wait_ge(pe_group, NS - 1 + RING)
            sp.wait_ge(dve_group, NS - 1 + RING)
            sp.wait_ge(o_out, 16)
            sp.dma_start(o_back, o_dram).then_inc(o_again, 16)

            sp.wait_ge(in_acc, (NS - 1) * Q + Q_LAST + 4)
            sp.wait_ge(dve_group, NS + RING)
            for h in range(H):
                sp.dma_start(recip[h * CH:(h + 1) * CH, :],
                             acc[h * HD:h * HD + 1, 1, :].rearrange("p (c n) -> p c n", c=CH)).then_inc(den_rows, 16)

            def store_out(g, k):
                sp.wait_ge(y_done, g + 1)
                if isinstance(g, int) and g == NG - 1:
                    first = g * 4 * P
                    sp.dma_start(out[first:N, :], x_sb[0:N - first, g * 4, :]).then_inc(y_out, 16)
                else:
                    sp.dma_start(out[bass.ds(g * 4 * P, 4 * P), :].rearrange("(i p) f -> p i f", p=P),
                                 x_sb[:, bass.ds(g * 4, 4), :]).then_inc(y_out, 16)
            node_groups(sp, store_out)
            sp.wait_ge(y_out, 16 * NG)

        @block.gpsimd
        def _(pool):
            nc.gpsimd.memset(ident[:, :], 0.0).then_inc(consts_step, 1)
            nc.gpsimd.memset(head_block[:, :], 1.0).then_inc(consts_step, 1)
            nc.gpsimd.memset(ones[:, :], 1.0).then_inc(consts_done, 1)
            nc.gpsimd.memset(eps_col[:, :], EPS).then_inc(consts_done, 1)
            nc.gpsimd.iota(iota_i[:, :], [[1, WIN]], base=0, channel_multiplier=0).then_inc(consts_done, 1)
            nc.gpsimd.memset(new_seg[:, :], 0.0).then_inc(consts_done, 1)
            nc.gpsimd.memset(spread[:, :], 0.0).then_inc(consts_done, 1)
            pool.wait_ge(consts_step, 2)
            nc.gpsimd.affine_select(out=ident[:, :], in_=ident[:, :], compare_op=ALU.not_equal, fill=1.0, base=0,
                                    pattern=[[-1, P]], channel_multiplier=1).then_inc(consts_done, 1)
            hb = head_block[:, :].rearrange("p (h d) -> p h d", h=H)
            nc.gpsimd.affine_select(out=hb, in_=hb, compare_op=ALU.is_ge, fill=0.0, base=0,
                                    pattern=[[-HD, H], [0, HD]], channel_multiplier=1).then_inc(consts_step, 1)
            pool.wait_ge(consts_step, 3)
            nc.gpsimd.affine_select(out=hb, in_=hb, compare_op=ALU.is_ge, fill=0.0, base=HD - 1,
                                    pattern=[[HD, H], [0, HD]], channel_multiplier=-1).then_inc(consts_done, 1)

            def keep(g, k):
                pool.wait_ge(ht_done, g + 1)
                pool.sem_inc(passed_pool, 1)
                w = tiles_of(g) * P
                nc.gpsimd.tensor_copy(h_t[:, bass.ds(g * 4 * P, w)], ht_ring[:, k, 0:w]).then_inc(ht_kept, 1)
            node_groups(pool, keep)

            def gather(it, r, windows, after, after2):
                s = it * RING + r
                pool.wait_ge(ints_ready[r], it * 16 + 16)
                pool.wait_ge(pe_group, s + 1)
                if r > 0:
                    pool.wait_ge(o_out, 16)
                pool.sem_inc(passed_pool, 1)
                for q in range(windows):
                    for j in range(q * QT, q * QT + QT):
                        pool.indirect_dma_start(
                            out=rows[:, r, j, :], out_offset=None, in_=table,
                            in_offset=bass.IndirectOffsetOnAxis(
                                ap=ints_sb[:, r, SRC_COLS.start + j:SRC_COLS.start + j + 1], axis=0),
                        ).then_inc(gathered[r][q], 16)

            pool.wait_ge(table_out, 16 * NG)
            rounds(pool, gather)

            pool.wait_ge(pe_group, NS - 1 + RING)
            nc.gpsimd.memset(back_sel, 0.0).then_inc(sel_zero, 1)
            pool.wait_ge(sel_zero, 1)
            bs = back_sel.rearrange("m (c f) -> m c f", c=CH)
            for h in range(H):
                nc.gpsimd.affine_select(out=bs[:, :, h * HD:(h + 1) * HD], in_=bs[:, :, h * HD:(h + 1) * HD],
                                        compare_op=ALU.not_equal, fill=1.0, base=-h * CH,
                                        pattern=[[-1, CH], [0, HD]], channel_multiplier=1).then_inc(sel_done, 1)

            def finish(g, k):
                t = tiles_of(g)
                xs = x_sb[:, bass.ds(g * 4, t), :]
                rs = res[:, bass.ds(g * 4, t), :]
                pool.wait_ge(normed, g + 1)
                pool.sem_inc(passed_pool, 1)
                nc.gpsimd.tensor_tensor(rs, rs, ga_row[:, :].unsqueeze(1).to_broadcast([P, t, D]),
                                        ALU.mult).then_inc(f_gamma, 1)
                pool.wait_ge(f_gamma, g + 1)
                pool.sem_inc(passed_pool, 1)
                nc.gpsimd.tensor_tensor(xs, xs, rs, ALU.add).then_inc(y_done, 1)
            node_groups(pool, finish)

        @block.scalar
        def _(act):
            act.dma_start(proj_sb[:, 0:D + ED], w_proj).then_inc(w_loaded, 16)
            act.dma_start(proj_sb[:, D + ED:D + 2 * ED], w_proj[:, D:D + ED]).then_inc(w_loaded, 16)
            act.dma_start(wout_sb[:, :], w_out).then_inc(w_loaded, 16)
            act.dma_start(b_col[:, :], b_proj.rearrange("(p a) -> p a", a=1)).then_inc(w_loaded, 16)
            act.dma_start(a_col[:, :], attn.rearrange("h (d a) -> (h d) a", a=1)).then_inc(w_loaded, 16)
            act.dma_start(x_sb[:, 8:24, :], xr[:, 8:24, :]).then_inc(x_middle, 16)
            act.dma_start(x_sb[:, 24:NT, :], xr[:, 24:NT, :]).then_inc(x_rest, 16)
            act.wait_ge(consts_done, 2)

            def node_part(g, k):
                if there(g):
                    act.wait_ge(mv4_done, g * 4 + tiles_of(g))
                    nc.scalar.activation(std4[:, k, :], mv4[:, k, :, 1], ACT.Sqrt, bias=eps_col[:, :]).then_inc(std_done, 1)
                if there(g - 2):
                    if not (isinstance(g, int) and g < 4):
                        act.wait_ge(ht_kept, g - 3)
                        act.wait_ge(tb_psum, g - 3)
                    act.wait_ge(ht_psum, g - 1)
                    w = tiles_of(g - 2) * P
                    nc.scalar.copy(ht_ring[:, k, 0:w], turn_psum(k)[:, 0:w]).then_inc(ht_done, 1)
                if there(g - 1):
                    act.wait_ge(ln_done, g)
                    for j in range(tiles_of(g - 1)):
                        i = (g - 1) * 4 + j
                        last = nc.scalar.activation(h_ring[:, 1 - k, j, :], tile(x_sb, i), ACT.Relu,
                                                    bias=shift[:, bass.ds(i, 1)], scale=rstd[:, bass.ds(i, 1)])
                    last.then_inc(h_done, 1)
            node_groups(act, node_part, lag=2)
            act.wait_ge(tb_psum, NG)

            def bring_back(g, k):
                act.wait_ge(ht_kept, NG)
                if not (isinstance(g, int) and g < 2):
                    act.wait_ge(o_pre_psum, g - 1)
                w = tiles_of(g) * P
                nc.scalar.copy(ht_ring[:, k, 0:w], h_t[:, bass.ds(g * 4 * P, w)]).then_inc(ht_again, 1)
            node_groups(act, bring_back)
            act.wait_ge(o_pre, NG)
            act.dma_start(o_dram, o_sb).then_inc(o_out, 16)

            def exps(s, r, windows):
                act.wait_ge(added, s * Q + windows)
                nc.scalar.copy(logit[:, :, :], rows[:, r, :, D:ROW].rearrange("p j h -> p h j")).then_inc(packed, 1)
                act.wait_ge(decay_in, s + 1)
                act.wait_ge(rescaled, s + 1)
                nc.scalar.activation(decay[:, :], decay_log[:, :], ACT.Exp).then_inc(decay_done, 1)
                act.wait_ge(centred_done, s + 1)
                nc.scalar.activation(ex[:, r, :, :], centred[:, :, :], ACT.Exp).then_inc(ex_done, 1)

            exps(0, 0, Q)

            def group(it, r, windows, after, after2):
                if after:
                    exps(it * RING + r + 1, (r + 1) % RING, after)

            rounds(act, group)

            def final_part(g, k):
                if there(g - 1):
                    rs = res[:, bass.ds((g - 1) * 4, tiles_of(g - 1)), :]
                    act.wait_ge(o_added, g)
                    nc.scalar.activation(rs, rs, ACT.Relu).then_inc(relu_done, 1)
                if there(g - 2):
                    act.wait_ge(f_mv4, (g - 2) * 4 + tiles_of(g - 2))
                    nc.scalar.activation(std4[:, k, :], mv4[:, k, :, 1], ACT.Sqrt, bias=eps_col[:, :]).then_inc(f_std, 1)
                if there(g - 3):
                    act.wait_ge(f_ln, g - 2)
                    for j in range(tiles_of(g - 3)):
                        i = (g - 3) * 4 + j
                        last = nc.scalar.activation(tile(res, i), tile(res, i), ACT.Identity,
                                                    bias=shift[:, bass.ds(i, 1)], scale=rstd[:, bass.ds(i, 1)])
                    last.then_inc(normed, 1)
            node_groups(act, final_part, lag=3)

        @block.tensor
        def _(pe):
            pe.sem_inc(pe_group, RING)
            pe.sem_inc(pair_done, 2)

            def weights():
                pe.wait_ge(set_ready, 3)
                nc.tensor.matmul(ps_a[:, 0, 0, 0:ROW], proj_sb[:, 0:D], rhs_set[:, :], start=True, stop=True).then_inc(set_mm, 1)
                nc.tensor.matmul(ps_a[:, 0, 1, 0:ROW], proj_sb[:, D:D + 2 * ED], rhs_set[:, :], start=True, stop=True).then_inc(set_mm, 1)
                nc.tensor.matmul(ps_a[:, 1, 0, 0:ROW], b_rep[:, :], rhs_set[:, :], start=True, stop=True).then_inc(set_mm, 1)
                nc.tensor.matmul(ps_a[:, 1, 1, 0:D], wout_sb[:, :], ident[:, :], start=True, stop=True).then_inc(set_mm, 1)
                pe.wait_ge(weights_done, 4)

            def node_part(g, k):
                if there(g - 2):
                    pe.wait_ge(ht_done, g - 1)
                    if not (isinstance(g, int) and g < 4):
                        pe.wait_ge(tb_done, g - 3)
                    for j in range(tiles_of(g - 2)):
                        last = nc.tensor.matmul(table_psum(k)[:, j // 2, (j % 2) * ROW:(j % 2 + 1) * ROW],
                                                ht_ring[:, k, j * P:(j + 1) * P], w_node[:, :], start=True, stop=True)
                    last.then_inc(tb_psum, 1)
                if there(g - 1):
                    pe.wait_ge(h_done, g)
                    if not (isinstance(g, int) and g < 3):
                        pe.wait_ge(ht_done, g - 2)
                    for j in range(tiles_of(g - 1)):
                        last = nc.tensor.transpose(turn_psum(1 - k)[:, j * P:(j + 1) * P], h_ring[:, 1 - k, j, :], ident[:, :])
                    last.then_inc(ht_psum, 1)
            node_groups(pe, node_part, lag=2, before={1: weights})

            def pre_output(g, k):
                pe.wait_ge(ht_again, g + 1)
                if not (isinstance(g, int) and g < 2):
                    pe.wait_ge(o_pre, g - 1)
                for j in range(tiles_of(g)):
                    last = nc.tensor.matmul(ps_c[:, k, j * P:(j + 1) * P], ht_ring[:, k, j * P:(j + 1) * P],
                                            w_out_t[:, :], start=True, stop=True)
                last.then_inc(o_pre_psum, 1)
            node_groups(pe, pre_output)
            pe.wait_ge(o_pre, NG)
            pe.wait_ge(tb_done, NG)

            def project(n, q, r, it):
                if q == 0:
                    pe.wait_ge(ee_ready[r], it * 16 + 16)
                if not (isinstance(n, int) and n < 2):
                    pe.wait_ge(added, n - 1)
                for j in (0, 2, 1, 3):
                    half = j // 2
                    t = q * 2 + j % 2
                    last = nc.tensor.matmul(ps_a[:, q % 2, half, (j % 2) * ROW:(j % 2 + 1) * ROW],
                                            ee_sb[half * ED:(half + 1) * ED, r, t * P:(t + 1) * P],
                                            w_edge[half * ED:(half + 1) * ED, :], start=True, stop=True)
                last.then_inc(projected, 1)

            for q in range(Q):
                project(q, q, 0, 0)

            passes = pe.alloc_register("pe_passes")
            pe.reg_mov(passes, 0)

            def turn_logits(s):
                pe.wait_ge(packed, s + 1)
                nc.tensor.transpose(e_t, logit[:, :, :].rearrange("p h j -> p (h j)"), ident[:, :]).then_inc(e_turned, 1)

            def spread_bounds(s):
                pe.wait_ge(spread_done, s + 1)
                nc.tensor.matmul(bounds_max, head_block[:, :], spread[:, :], start=True, stop=True).then_inc(bounds_done, 1)

            def turn_maxima(s):
                pe.wait_ge(max_done, s + 1)
                nc.tensor.transpose(max_back, seg_max[:, :], ident[:, :]).then_inc(max_turned, 1)

            turn_logits(0)
            spread_bounds(0)
            turn_maxima(0)
            project(Q, 0, 1, 0)
            project(Q + 1, 1, 1, 0)

            def group(it, r, windows, after, after2):
                s = it * RING + r
                r1, it1 = (r + 1) % RING, it + (r + 1) // RING
                r2, it2 = (r + 2) % RING, it + (r + 2) // RING
                pe.wait_ge(span_done, s + 1)
                for q in range(windows):
                    n = s * Q + q
                    if q == windows - 1 and after:
                        turn_logits(s + 1)
                    pe.wait_ge(sum_done, n + 2)
                    if q % 2 == 0:
                        pe.wait_ge(in_acc, n + 2)
                    window(r, q, q % 4, (q // 2) % 2)
                    if q % 2 or q == windows - 1:
                        window_den(q - q % 2, 1 + q % 2, (q // 2) % 2).then_inc(pair_done, 1)
                    if q + 2 < after:
                        project((s + 1) * Q + q + 2, q + 2, r1, it1)
                if after:
                    spread_bounds(s + 1)
                if after2:
                    project((s + 2) * Q, 0, r2, it2)
                width = pe.value_load(span[0:1, r:r + 1], min_val=0, max_val=NPAD)
                if after:
                    turn_maxima(s + 1)
                if after2:
                    project((s + 2) * Q + 1, 1, r2, it2)
                with pe.If(width >= WIN):
                    with pe.Fori(WIN, width + 1, WIN):
                        done = pe.snap(passes, min_val=0, max_val=NS * NPAD)
                        for q in range(Q):
                            pe.wait_ge(x_sum, done * Q + q + 1)
                            window(r, q, q % 2, 0)
                            window_den(q, 1, 0).then_inc(x_agg, 1)
                        pe.reg_add(passes, passes, 1)
                pe.drain().then_inc(pe_group, 1)

            def window(r, q, k, bank):
                first = (q % 2) * H * WIN
                for j in range(QT):
                    nc.tensor.matmul(ps_c[:, bank, first:first + H * WIN], rows[:, r, q * QT + j, 0:D],
                                     sx[:, k, j, :, :].rearrange("p h n -> p (h n)"), start=j == 0, stop=j == QT - 1)

            def window_den(q, count, bank):
                first = (2 + q % 2) * H * WIN
                return nc.tensor.matmul(ps_c[:, bank, first:first + count * H * WIN], ones[:, :],
                                        sx_sum[:, bank, q % 2:q % 2 + count, :, :].rearrange("p w h n -> p (w h n)"),
                                        start=True, stop=True)

            rounds(pe, group)

            pe.wait_ge(recip_done, 1)
            pe.wait_ge(sel_done, H)

            def out_part(g):
                if g < NG:
                    if g >= 2:
                        pe.wait_ge(z_done, g - 1)
                    for first in range(0, tiles_of(g) * P, DC):
                        c = (g * 4 * P + first) // DC
                        w = min(DC, tiles_of(g) * P - first)
                        last = nc.tensor.matmul(ps_a[:, g % 2, 1, first:first + w], back_sel[:, c * P:(c + 1) * P],
                                                recip[:, 0:w], start=True, stop=True)
                    last.then_inc(rec_psum, 1)
                if g >= 1:
                    k = (g - 1) % 2
                    pe.wait_ge(z_done, g)
                    if g >= 3:
                        pe.wait_ge(o_added, g - 2)
                    for j in range(tiles_of(g - 1)):
                        last = nc.tensor.matmul(ps_a[:, k, 0, j * P:(j + 1) * P], z_buf[:, k, j * P:(j + 1) * P],
                                                w_out_t[:, :], start=True, stop=True)
                    last.then_inc(o_psum, 1)

            for g in range(NG + 1):
                out_part(g)

        @block.vector
        def _(dve):
            v = nc.vector

            def hold(what, value):
                dve.wait_ge(what, value)
                dve.sem_inc(passed, 1)

            dve.sem_inc(dve_group, RING)
            dve.sem_inc(in_acc, 4)
            dve.sem_inc(sum_done, 1)
            dve.sem_inc(rescaled, 1)

            def weights():
                dve.wait_ge(consts_done, 7)
                dve.wait_ge(w_loaded, 16 * 8)
                v.tensor_copy(iota_f[:, :], iota_i[:, :]).then_inc(set_step, 1)
                v.tensor_copy(rhs_set[:, 0:D], ident[:, :]).then_inc(set_ready, 1)
                v.tensor_scalar(rhs_set[:, D:ROW], head_block[:, :].rearrange("p (h d) -> p h d", h=H)[:, :, 0],
                                a_col[:, 0:1], None, ALU.mult).then_inc(set_ready, 1)
                v.tensor_scalar(b_rep[:, :], ones[:, :], b_col[:, 0:1], None, ALU.mult).then_inc(set_ready, 1)
                v.tensor_reduce(diag[:, :], ident[:, :].rearrange("p (h k) -> p k h", h=H), AX_X, ALU.add).then_inc(set_step, 1)
                dve.wait_ge(set_mm, 4)
                v.tensor_copy(w_node[:, :], ps_a[:, 0, 0, 0:ROW]).then_inc(weights_done, 1)
                v.tensor_copy(w_edge[:, :], ps_a[:, 0, 1, 0:ROW]).then_inc(weights_done, 1)
                v.tensor_copy(bias_row[:, :], ps_a[:, 1, 0, 0:ROW]).then_inc(weights_done, 1)
                v.tensor_copy(w_out_t[:, :], ps_a[:, 1, 1, 0:D]).then_inc(weights_done, 1)
                hold(weights_done, 4)

            def moments(src, g, k, stats_sem, mv_sem):
                for j in range(tiles_of(g)):
                    v.bn_stats(stats[:, k, j, :], tile(src, g * 4 + j)).then_inc(stats_sem, 1)
                hold(stats_sem, g * 4 + tiles_of(g))
                for j in range(tiles_of(g)):
                    v.bn_aggr(mv4[:, k, j, :], stats[:, k, j, :]).then_inc(mv_sem, 1)

            def scale_shift(g, k, std_sem, rstd_sem, ln_sem):
                dve.wait_ge(std_sem, g + 1)
                v.reciprocal(rstd[:, bass.ds(g * 4, 4)], std4[:, k, :]).then_inc(rstd_sem, 1)
                dve.wait_ge(rstd_sem, g + 1)
                v.scalar_tensor_tensor(out=shift[:, bass.ds(g * 4, 4)], in0=mv4[:, k, :, 0], scalar=-1.0,
                                       in1=rstd[:, bass.ds(g * 4, 4)], op0=ALU.mult, op1=ALU.mult).then_inc(ln_sem, 1)

            def node_part(g, k):
                if there(g):
                    moments(x_sb, g, k, stats_done, mv4_done)
                if there(g - 3):
                    dve.wait_ge(tb_psum, g - 2)
                    if tiles_of(g - 3) == 4:
                        v.tensor_tensor(table_sb[:, bass.ds((g - 3) * 4, 4), :].rearrange("p (a b) c -> p a (b c)", a=2),
                                        table_psum(1 - k),
                                        bias_row[:, :].unsqueeze(1).to_broadcast([P, 4, ROW]).rearrange("p (a b) c -> p a b c", a=2),
                                        ALU.add).then_inc(tb_done, 1)
                    else:
                        v.tensor_tensor(table_sb[:, (g - 3) * 4, :], table_psum(1 - k)[:, 0, 0:ROW], bias_row[:, :],
                                        ALU.add).then_inc(tb_done, 1)
                if there(g):
                    scale_shift(g, k, std_done, rstd_step, ln_done)

            def middle():
                dve.wait_ge(x_middle, 16)

            def rest():
                dve.wait_ge(x_rest, 16)
            dve.wait_ge(x_first, 16)
            node_groups(dve, node_part, lag=3, before={1: weights, 2: middle, 4: rest})

            def pre_output(g, k):
                dve.wait_ge(o_pre_psum, g + 1)
                t = tiles_of(g)
                v.tensor_tensor(o_sb[:, bass.ds(g * 4 * P, t * P)].rearrange("p (j f) -> p j f", j=t),
                                ps_c[:, k, 0:t * P].rearrange("p (j f) -> p j f", j=t),
                                bo_row[:, :].unsqueeze(1).to_broadcast([P, t, D]), ALU.add).then_inc(o_pre, 1)
            dve.wait_ge(table_out, 16 * NG)
            node_groups(dve, pre_output)
            dve.wait_ge(ht_again, NG)
            v.memset(acc[:, :, :], 0.0).then_inc(acc_zero, 1)
            v.tensor_tensor(x_sb[:, :, :], x_sb[:, :, :], be_row[:, :].unsqueeze(1).to_broadcast([P, NT, D]),
                            ALU.add).then_inc(x_beta, 1)
            dve.wait_ge(acc_zero, 1)
            dve.wait_ge(set_step, 2)

            def add_rows(n, q, r, it):
                dve.wait_ge(projected, n + 1)
                dve.wait_ge(gathered[r][q], it * 16 * QT + 16 * QT)
                g = rows[:, r, q * QT:(q + 1) * QT, :].rearrange("p (a b) c -> p a (b c)", a=2)
                v.tensor_tensor(g, g, ps_a[:, q % 2, :, 0:2 * ROW], ALU.add).then_inc(added, 1)

            for q in range(Q):
                add_rows(q, q, 0, 0)

            passes = dve.alloc_register("dve_passes")
            dve.reg_mov(passes, 0)
            at = dve.alloc_register("extra_node")

            def make_hot(r, done):
                v.tensor_tensor(one_hot[:, r, :, :], iota_f[:, :].unsqueeze(1).to_broadcast([P, GT, WIN]),
                                dst_rel[:, r, :].unsqueeze(2).to_broadcast([P, GT, WIN]), ALU.is_equal).then_inc(done, 1)

            def make_sx(r, q, k, done):
                v.tensor_tensor(sx[:, k, :, :, :],
                                one_hot[:, r, q * QT:(q + 1) * QT, :].unsqueeze(2).to_broadcast([P, QT, H, WIN]),
                                ex[:, r, :, q * QT:(q + 1) * QT].rearrange("p h t -> p t h").unsqueeze(3).to_broadcast([P, QT, H, WIN]),
                                ALU.mult).then_inc(done, 1)

            def sum_sx(k, done):
                v.tensor_reduce(sx_sum[:, k // 2, k % 2, :, :], sx[:, k, :, :, :].rearrange("p t h n -> p h n t"),
                                AX_X, ALU.add).then_inc(done, 1)

            def drain(k, node, done):
                for h in range(H):
                    mine = slice(h * HD, (h + 1) * HD)
                    first = (k % 2) * H * WIN + h * WIN
                    a = acc[mine, :, bass.ds(node, WIN)]
                    last = v.tensor_tensor(a, a, ps_c[mine, k // 2, 0:4 * H * WIN].rearrange(
                        "p (a b) -> p a b", a=2)[:, :, first:first + WIN], ALU.add)
                last.then_inc(done, 1)

            def first_node(r, q):
                base = P + 2 * GT + q * 2 * QT
                return dve.value_load(ints_sb[0:1, r, base:base + 1], min_val=0, max_val=PAD_DST)

            def add_windows(s, r, first, last):
                for q in range(first, last):
                    node = first_node(r, q)
                    if q % 2 == 0:
                        dve.wait_ge(pair_done, s * (Q // 2) + q // 2 + 3)
                    dve.wait_ge(in_acc, s * Q + q + 4)
                    if q == 0:
                        dve.wait_ge(rescaled, s + 2)
                    drain(q % 4, node, in_acc)

            def prepare(s, it, r, windows):
                iv = ints_sb[:, r, :]
                dve.wait_ge(ints_ready[r], it * 16 + 16)
                v.tensor_scalar(dst_s[:, :], iv[:, DST_ROWS], 1e30, None, ALU.mult).then_inc(scaled, 1)
                v.tensor_scalar(bnd_s[:, :], iv[:, BOUNDS], 1e30, None, ALU.mult).then_inc(scaled, 1)
                tile_bounds = iv[:, BOUNDS][:, 0:2 * GT].rearrange("p (q c) -> p q c", q=Q)
                v.tensor_tensor(spans[0:1, :], tile_bounds[0:1, :, 2 * QT - 1], tile_bounds[0:1, :, 0],
                                ALU.subtract).then_inc(spans_done, 1)
                v.tensor_tensor(dst_rel[:, r, :].rearrange("p (q t) -> p q t", q=Q),
                                iv[:, DST_COLS].rearrange("p (q t) -> p q t", q=Q),
                                tile_bounds[:, :, 0:1].to_broadcast([P, Q, QT]), ALU.subtract).then_inc(rel_done, 1)
                dve.wait_ge(scaled, s * 2 + 2)
                v.tensor_tensor(new_seg[:, 1:P], dst_s[:, 0:P - 1], dst_s[:, 1:P], ALU.subtract).then_inc(masked, 1)
                v.tensor_scalar(not_first[:, :], dst_s[:, :], dst_s[:, 0:1], NEG, ALU.not_equal, ALU.mult).then_inc(masked, 1)
                v.tensor_scalar(not_last[:, :], dst_s[:, :], dst_s[:, P - 1:P], NEG, ALU.not_equal, ALU.mult).then_inc(masked, 1)
                for m, node in enumerate((dst_s[:, 0:1], dst_s[:, P - 1:P], bnd_s[:, NB - 1:NB])):
                    v.tensor_scalar(nb_masks[:, m, :], bnd_s[:, :], node, NEG, ALU.not_equal, ALU.mult).then_inc(masked, 1)
                dve.wait_ge(spans_done, s + 1)
                v.tensor_reduce(span[:, r:r + 1], spans[:, :], AX_X, ALU.max).then_inc(span_done, 1)
                dve.wait_ge(span_done, s + 1)
                dve.wait_ge(rel_done, s + 1)
                make_hot(r, hot_done)

            def local_maxima(s):
                dve.wait_ge(masked, s * 6 + 6)
                hold(e_turned, s + 1)
                for m, mask in enumerate((not_first, not_last)):
                    v.tensor_tensor_reduce(junk[:, m, :], e_t, mask[:, :], 1.0, 0.0, ALU.add, ALU.max,
                                           local[:, m:m + 1]).then_inc(local_done, 1)
                dve.wait_ge(local_done, s * 2 + 2)
                v.tensor_tensor(spread[:, 0:2 * GT].rearrange("p (t m) -> p t m", m=2),
                                diag[:, :].unsqueeze(2).to_broadcast([P, GT, 2]),
                                local[:, :].unsqueeze(1).to_broadcast([P, GT, 2]), ALU.mult).then_inc(spread_done, 1)

            def segment_maxima(s):
                hold(bounds_done, s + 1)
                for m in range(3):
                    v.tensor_tensor_reduce(junk_bounds[:, m, :], bounds_max, nb_masks[:, m, :], 1.0, 0.0, ALU.add, ALU.max,
                                           full[:, m:m + 1]).then_inc(full_done, 1)
                hold(full_done, s * 3 + 3)
                v.tensor_tensor_scan(fwd[:, :], new_seg[:, 0:P], e_t, full[:, 0:1], ALU.add, ALU.max).then_inc(fwd_done, 1)
                v.tensor_tensor(spread[:, NB - 1:NB], full[:, 1:2], diag[:, GT - 1:GT], ALU.mult).then_inc(carry_done, 1)
                v.tensor_tensor(decay_log[:, :], bounds_max[:, NB - 1:NB], full[:, 2:3], ALU.subtract).then_inc(decay_in, 1)
                dve.wait_ge(fwd_done, s + 1)
                v.tensor_tensor_scan(seg_max[:, ::-1], new_seg[:, 1:P + 1][:, ::-1], fwd[:, ::-1], full[:, 1:2],
                                     ALU.add, ALU.max).then_inc(max_done, 1)

            def centre(s):
                dve.wait_ge(max_turned, s + 1)
                v.tensor_tensor(centred[:, :, :], logit[:, :, :], max_back.rearrange("p (h j) -> p h j", h=H),
                                ALU.subtract).then_inc(centred_done, 1)

            def spread_ex(s, r, q, after, r1, it1):
                if q % 2 == 0:
                    dve.wait_ge(pair_done, s * (Q // 2) + q // 2 + 1)
                make_sx(r, q, q % 4, sx_done)
                dve.wait_ge(sx_done, s * Q + q + 1)
                sum_sx(q % 4, sum_done)
                for w in {Q - 2: (Q - 2, Q - 1), Q - 1: ()}.get(q, (q,)):
                    if w < after:
                        add_rows((s + 1) * Q + w, w, r1, it1)

            def start_group(s, it, r, after):
                dve.wait_ge(ex_done, s + 1)
                dve.wait_ge(hot_done, s + 1)
                for q in range(2):
                    spread_ex(s, r, q, after, (r + 1) % RING, it + (r + 1) // RING)
                if not isinstance(s, int) or s > 0:
                    add_windows(s - 1, (r - 1) % RING, Q - 2, Q)
                node = dve.value_load(ints_sb[0:1, r, NI - 1:NI], min_val=0, max_val=LEAD_DST)
                dve.wait_ge(decay_done, s + 1)
                dve.wait_ge(in_acc, s * Q + 4)
                carried = acc[:, :, bass.ds(node, 1)]
                v.tensor_scalar(carried, carried, decay[:, 0:1], None, ALU.mult).then_inc(rescaled, 1)

            prepare(0, 0, 0, Q)
            local_maxima(0)
            segment_maxima(0)
            centre(0)
            start_group(0, 0, 0, Q)

            def group(it, r, windows, after, after2):
                s = it * RING + r
                r1, it1 = (r + 1) % RING, it + (r + 1) // RING
                for q in range(2, windows):
                    spread_ex(s, r, q, after, r1, it1)
                    if q == 2 and after:
                        prepare(s + 1, it1, r1, after)
                    if q % 2:
                        add_windows(s, r, q - 3, q - 1)
                if after:
                    local_maxima(s + 1)
                    segment_maxima(s + 1)
                else:
                    add_windows(s, r, 0, windows)
                width = dve.value_load(span[0:1, r:r + 1], min_val=0, max_val=NPAD)
                if after:
                    centre(s + 1)
                with dve.If(width >= WIN):
                    with dve.Fori(WIN, width + 1, WIN) as off:
                        done = dve.snap(passes, min_val=0, max_val=NS * NPAD)
                        dve.wait_ge(in_acc, s * Q + (Q - 2 if after else windows) + 4)
                        v.tensor_scalar(dst_rel[:, r, :], dst_rel[:, r, :], -float(WIN), None, ALU.add).then_inc(x_rel, 1)
                        dve.wait_ge(x_rel, done + 1)
                        make_hot(r, x_hot)
                        dve.wait_ge(x_hot, done + 1)
                        for q in range(Q):
                            make_sx(r, q, q % 2, x_sx)
                            dve.wait_ge(x_sx, done * Q + q + 1)
                            sum_sx(q % 2, x_sum)
                            node = first_node(r, q)
                            dve.wait_ge(x_agg, done * Q + q + 1)
                            dve.reg_alu(at, node + off, NPAD - WIN, ALU.min)
                            drain(q % 2, dve.snap(at, min_val=0, max_val=NPAD - WIN), x_drained)
                            dve.wait_ge(x_drained, done * Q + q + 1)
                        dve.reg_add(passes, passes, 1)
                if after:
                    start_group(s + 1, it1, r1, after2)
                dve.drain().then_inc(dve_group, 1)

            rounds(dve, group)

            dve.wait_ge(den_rows, 16 * H)
            v.tensor_scalar(recip, recip, 1e-30, None, ALU.max).then_inc(den_safe, 1)
            dve.wait_ge(den_safe, 1)
            v.reciprocal(recip, recip).then_inc(recip_done, 1)
            dve.wait_ge(o_again, 16)
            dve.wait_ge(x_beta, 1)

            def final_part(g, k):
                if there(g):
                    w = tiles_of(g) * P
                    cols = bass.ds(g * 4 * P, w)
                    dve.wait_ge(rec_psum, g + 1)
                    if not (isinstance(g, int) and g < 2):
                        dve.wait_ge(o_psum, g - 1)
                    v.tensor_tensor(z_buf[:, k, 0:w], acc[:, 0, cols], ps_a[:, k, 1, 0:w], ALU.mult).then_inc(z_done, 1)
                if there(g - 1):
                    dve.wait_ge(o_psum, g)
                    t = tiles_of(g - 1)
                    v.tensor_tensor(res[:, bass.ds((g - 1) * 4, t), :],
                                    ps_a[:, 1 - k, 0, 0:t * P].rearrange("p (j f) -> p j f", j=t),
                                    o_back[:, bass.ds((g - 1) * 4 * P, t * P)].rearrange("p (j f) -> p j f", j=t),
                                    ALU.add).then_inc(o_added, 1)
                if there(g - 2):
                    hold(relu_done, g - 1)
                    moments(res, g - 2, k, f_stats, f_mv4)
                if there(g - 3):
                    scale_shift(g - 3, 1 - k, f_std, f_rstd, f_ln)
            node_groups(dve, final_part, lag=3)


def kernel(x, src, dst, edge_attr_64, L0_gnn_W_proj_w, L0_gnn_W_proj_b, L0_gnn_attn_vec, L0_gnn_W_out_w,
           L0_gnn_W_out_b, L0_gnn_ln_gamma, L0_gnn_ln_beta):
    import numpy as np
    import concourse.bacc as bacc
    from concourse.bass_utils import run_bass_kernel_spmd

    edges = NS * GT * P
    src, dst = np.asarray(src), np.asarray(dst)
    src_p = np.zeros(edges, src.dtype)
    src_p[:E] = src
    dst_p = np.full(edges, PAD_DST, dst.dtype)
    dst_p[:E] = dst
    src_t = src_p.reshape(NS, GT, P)
    dst_t = dst_p.reshape(NS, GT, P)
    before = np.concatenate([np.full(1, LEAD_DST, dst.dtype), dst_t[:-1, -1, -1]])
    bounds = np.concatenate([dst_t[:, :, [0, P - 1]].reshape(NS, 2 * GT), before[:, None]], axis=1)
    ints = np.concatenate([
        np.tile(dst_t, (1, H, 1)),
        dst_t.transpose(0, 2, 1),
        src_t.transpose(0, 2, 1),
        np.broadcast_to(bounds[:, None, :], (NS, P, NB)),
    ], axis=2)
    ee = np.asarray(edge_attr_64)
    ee_p = np.zeros((edges, ED), ee.dtype)
    ee_p[:E] = ee
    ee_t = ee_p.reshape(NS, Q, 2, QT // 2 * P, ED).transpose(0, 2, 4, 1, 3).reshape(NS, P, GT // 2 * P)
    x = np.asarray(x)
    x_p = np.zeros((NT * P, D), x.dtype)
    x_p[:N] = x
    arrays = {
        "x_in": x_p, "ints_in": ints, "ee_in": ee_t, "w_proj_in": L0_gnn_W_proj_w, "b_proj_in": L0_gnn_W_proj_b,
        "attn_in": L0_gnn_attn_vec, "w_out_in": L0_gnn_W_out_w, "b_out_in": L0_gnn_W_out_b,
        "gamma_in": L0_gnn_ln_gamma, "beta_in": L0_gnn_ln_beta,
    }
    arrays = {k: np.ascontiguousarray(a) for k, a in arrays.items()}
    nc = bacc.Bacc("TRN2", target_bir_lowering=False, num_devices=1)
    args = [nc.dram_tensor(k, a.shape, mybir.dt.from_np(a.dtype), kind="ExternalInput").ap() for k, a in arrays.items()]
    out = nc.dram_tensor("out", (N, D), F32, kind="ExternalOutput").ap()
    build(nc, *args, out)
    return run_bass_kernel_spmd(nc, [arrays], core_ids=[0]).results[0]["out"]
```
